# Optimizing a Trainium2 kernel written in Bass

```python
import numpy as np
import jax
import jax.numpy as jnp

def _softmax(x, axis=-1):
    return jax.nn.softmax(x, axis=axis)
def _gelu(x):
    return jax.nn.gelu(x, approximate=True)
def _silu(x):
    return jax.nn.silu(x)
def _sigmoid(x):
    return jax.nn.sigmoid(x)
def _layernorm(x, axis=-1, eps=1e-5):
    m = jnp.mean(x, axis=axis, keepdims=True)
    v = jnp.var(x, axis=axis, keepdims=True)
    return (x - m) / jnp.sqrt(v + eps)
def _scatter_add(tgt, idx, src, axis=0):
    return tgt.at[idx].add(src)
def _segment_sum(src, seg, n):
    return jax.ops.segment_sum(src, seg, n)

kernel_name = 'mk_rec_standalone_d1_rec_1d4277'

def setup_inputs(seed: int = 0):
    np.random.seed(seed)
    _w = jnp.asarray
    def _rec_inputs():
        import jax
        import jax.numpy as jnp
        _rk = jax.random.key(seed)
        r_dense_x = -0.00142785 + 1.00275 * jax.random.normal(jax.random.fold_in(_rk, 1), (1024, 13), jnp.float32)
        r_discrete_x = jnp.stack([jax.random.randint(jax.random.fold_in(jax.random.fold_in(_rk, 2), 0), (1024,), 2, 99993, jnp.int32), jax.random.randint(jax.random.fold_in(jax.random.fold_in(_rk, 2), 1), (1024,), 54, 99982, jnp.int32), jax.random.randint(jax.random.fold_in(jax.random.fold_in(_rk, 2), 2), (1024,), 14, 99989, jnp.int32), jax.random.randint(jax.random.fold_in(jax.random.fold_in(_rk, 2), 3), (1024,), 5, 99994, jnp.int32), jax.random.randint(jax.random.fold_in(jax.random.fold_in(_rk, 2), 4), (1024,), 20, 99974, jnp.int32), jax.random.randint(jax.random.fold_in(jax.random.fold_in(_rk, 2), 5), (1024,), 12, 99986, jnp.int32), jax.random.randint(jax.random.fold_in(jax.random.fold_in(_rk, 2), 6), (1024,), 24, 99984, jnp.int32), jax.random.randint(jax.random.fold_in(jax.random.fold_in(_rk, 2), 7), (1024,), 35, 99979, jnp.int32), jax.random.randint(jax.random.fold_in(jax.random.fold_in(_rk, 2), 8), (1024,), 0, 99954, jnp.int32), jax.random.randint(jax.random.fold_in(jax.random.fold_in(_rk, 2), 9), (1024,), 27, 99986, jnp.int32), jax.random.randint(jax.random.fold_in(jax.random.fold_in(_rk, 2), 10), (1024,), 4, 99976, jnp.int32), jax.random.randint(jax.random.fold_in(jax.random.fold_in(_rk, 2), 11), (1024,), 21, 99934, jnp.int32), jax.random.randint(jax.random.fold_in(jax.random.fold_in(_rk, 2), 12), (1024,), 20, 99960, jnp.int32), jax.random.randint(jax.random.fold_in(jax.random.fold_in(_rk, 2), 13), (1024,), 5, 99989, jnp.int32), jax.random.randint(jax.random.fold_in(jax.random.fold_in(_rk, 2), 14), (1024,), 2, 99987, jnp.int32), jax.random.randint(jax.random.fold_in(jax.random.fold_in(_rk, 2), 15), (1024,), 38, 99981, jnp.int32), jax.random.randint(jax.random.fold_in(jax.random.fold_in(_rk, 2), 16), (1024,), 0, 99998, jnp.int32), jax.random.randint(jax.random.fold_in(jax.random.fold_in(_rk, 2), 17), (1024,), 13, 99983, jnp.int32), jax.random.randint(jax.random.fold_in(jax.random.fold_in(_rk, 2), 18), (1024,), 48, 99965, jnp.int32), jax.random.randint(jax.random.fold_in(jax.random.fold_in(_rk, 2), 19), (1024,), 47, 99999, jnp.int32), jax.random.randint(jax.random.fold_in(jax.random.fold_in(_rk, 2), 20), (1024,), 4, 99975, jnp.int32), jax.random.randint(jax.random.fold_in(jax.random.fold_in(_rk, 2), 21), (1024,), 1, 99990, jnp.int32), jax.random.randint(jax.random.fold_in(jax.random.fold_in(_rk, 2), 22), (1024,), 1, 99994, jnp.int32), jax.random.randint(jax.random.fold_in(jax.random.fold_in(_rk, 2), 23), (1024,), 4, 99954, jnp.int32), jax.random.randint(jax.random.fold_in(jax.random.fold_in(_rk, 2), 24), (1024,), 6, 99998, jnp.int32), jax.random.randint(jax.random.fold_in(jax.random.fold_in(_rk, 2), 25), (1024,), 2, 99972, jnp.int32)], axis=1)
        return r_dense_x, r_discrete_x
    r_dense_x, r_discrete_x = _rec_inputs()
    def _L0_rec_setup():
        import jax, jax.numpy as jnp
        import numpy as np
        B, NS, DNS, D, V, F, HID = (4096, 26, 13, 16, 100000, 128, 1024)
        N = NS + DNS
        EPS = 1e-05

        def _bn_eval(x, g, b):
            return x * (g / jnp.sqrt(1.0 + EPS)) + b
        key = jax.random.key(seed)
        ks = jax.random.split(key, 32)
        s = 0.05
        d1, d2, d3 = (HID, HID // 2, HID // 4)
        din = NS * D + DNS
        return {'dense_x': jax.random.normal(ks[0], (B, DNS), jnp.float32), 'discrete_x': jax.random.randint(ks[1], (B, NS), 0, V, jnp.int32), 'lin_emb': jax.random.normal(ks[2], (NS, V, 1), jnp.float32) * s, 'emb_W': jax.random.normal(ks[3], (NS, V, D), jnp.float32) * s, 'dense_W': jax.random.normal(ks[4], (DNS, 1), jnp.float32) * s, 'dense_b': jnp.zeros((1,), jnp.float32), 'W1': jax.random.normal(ks[5], (din, d1), jnp.float32) * s, 'b1': jnp.zeros((d1,), jnp.float32), 'bn1_g': jnp.ones((d1,), jnp.float32), 'bn1_b': jnp.zeros((d1,), jnp.float32), 'W2': jax.random.normal(ks[6], (d1, d2), jnp.float32) * s, 'b2': jnp.zeros((d2,), jnp.float32), 'bn2_g': jnp.ones((d2,), jnp.float32), 'bn2_b': jnp.zeros((d2,), jnp.float32), 'W3': jax.random.normal(ks[7], (d2, d3), jnp.float32) * s, 'b3': jnp.zeros((d3,), jnp.float32), 'bn3_g': jnp.ones((d3,), jnp.float32), 'bn3_b': jnp.zeros((d3,), jnp.float32), 'Wout': jax.random.normal(ks[8], (d3, 1), jnp.float32) * s, 'bout': jnp.zeros((1,), jnp.float32), 'dense_proj': jax.random.normal(ks[9], (DNS, D), jnp.float32) * s, 'cin_W0': jax.random.normal(ks[10], (F, N, N), jnp.float32) * s, 'cin_W1': jax.random.normal(ks[11], (F, F, N), jnp.float32) * s, 'cin_W2': jax.random.normal(ks[12], (F, F, N), jnp.float32) * s, 'cin_out_W': jax.random.normal(ks[13], (3 * F, 1), jnp.float32) * s, 'cin_out_b': jnp.zeros((1,), jnp.float32)}
    _L0_rec_all = _L0_rec_setup()
    _L0_rec_in = {k: v for k, v in _L0_rec_all.items() if k in ('lin_emb', 'emb_W', 'dense_W', 'dense_b', 'W1', 'b1', 'bn1_g', 'bn1_b', 'W2', 'b2', 'bn2_g', 'bn2_b', 'W3', 'b3', 'bn3_g', 'bn3_b', 'Wout', 'bout', 'dense_proj', 'cin_W0', 'cin_W1', 'cin_W2', 'cin_out_W', 'cin_out_b', )}
    del _L0_rec_all

    return {
        "r_dense_x": r_dense_x,
        "r_discrete_x": r_discrete_x,
        "L0_rec_lin_emb": _L0_rec_in["lin_emb"],
        "L0_rec_emb_W": _L0_rec_in["emb_W"],
        "L0_rec_dense_W": _L0_rec_in["dense_W"],
        "L0_rec_dense_b": _L0_rec_in["dense_b"],
        "L0_rec_W1": _L0_rec_in["W1"],
        "L0_rec_b1": _L0_rec_in["b1"],
        "L0_rec_bn1_g": _L0_rec_in["bn1_g"],
        "L0_rec_bn1_b": _L0_rec_in["bn1_b"],
        "L0_rec_W2": _L0_rec_in["W2"],
        "L0_rec_b2": _L0_rec_in["b2"],
        "L0_rec_bn2_g": _L0_rec_in["bn2_g"],
        "L0_rec_bn2_b": _L0_rec_in["bn2_b"],
        "L0_rec_W3": _L0_rec_in["W3"],
        "L0_rec_b3": _L0_rec_in["b3"],
        "L0_rec_bn3_g": _L0_rec_in["bn3_g"],
        "L0_rec_bn3_b": _L0_rec_in["bn3_b"],
        "L0_rec_Wout": _L0_rec_in["Wout"],
        "L0_rec_bout": _L0_rec_in["bout"],
        "L0_rec_dense_proj": _L0_rec_in["dense_proj"],
        "L0_rec_cin_W0": _L0_rec_in["cin_W0"],
        "L0_rec_cin_W1": _L0_rec_in["cin_W1"],
        "L0_rec_cin_W2": _L0_rec_in["cin_W2"],
        "L0_rec_cin_out_W": _L0_rec_in["cin_out_W"],
        "L0_rec_cin_out_b": _L0_rec_in["cin_out_b"],
    }

def reference(r_dense_x, r_discrete_x, L0_rec_lin_emb, L0_rec_emb_W, L0_rec_dense_W, L0_rec_dense_b, L0_rec_W1, L0_rec_b1, L0_rec_bn1_g, L0_rec_bn1_b, L0_rec_W2, L0_rec_b2, L0_rec_bn2_g, L0_rec_bn2_b, L0_rec_W3, L0_rec_b3, L0_rec_bn3_g, L0_rec_bn3_b, L0_rec_Wout, L0_rec_bout, L0_rec_dense_proj, L0_rec_cin_W0, L0_rec_cin_W1, L0_rec_cin_W2, L0_rec_cin_out_W, L0_rec_cin_out_b):
    import jax
    import jax.numpy as jnp
    def _L0_rec_ref(dense_x, discrete_x, lin_emb, emb_W, dense_W, dense_b, W1, b1, bn1_g, bn1_b, W2, b2, bn2_g, bn2_b, W3, b3, bn3_g, bn3_b, Wout, bout, dense_proj, cin_W0, cin_W1, cin_W2, cin_out_W, cin_out_b):
        import jax, jax.numpy as jnp
        import numpy as np
        B, NS, DNS, D, V, F, HID = (4096, 26, 13, 16, 100000, 128, 1024)
        N = NS + DNS
        EPS = 1e-05

        def _bn_eval(x, g, b):
            return x * (g / jnp.sqrt(1.0 + EPS)) + b
        fld = jnp.arange(NS)
        linear_logits = dense_x @ dense_W + dense_b + lin_emb[fld, discrete_x].sum(axis=1)
        x_embeds = emb_W[fld, discrete_x]
        h = jnp.concatenate([x_embeds.reshape(x_embeds.shape[0], -1), dense_x], axis=1)
        h = jax.nn.relu(_bn_eval(h @ W1 + b1, bn1_g, bn1_b))
        h = jax.nn.relu(_bn_eval(h @ W2 + b2, bn2_g, bn2_b))
        h = jax.nn.relu(_bn_eval(h @ W3 + b3, bn3_g, bn3_b))
        dnn_logits = h @ Wout + bout
        x0 = jnp.concatenate([x_embeds, dense_x[:, :, None] * dense_proj], axis=1)
        xj = x0
        p_list = []
        for W in (cin_W0, cin_W1, cin_W2):
            cin_out = jnp.einsum('bcd,bnd,fcn->bfd', xj, x0, W)
            p_list.append(cin_out.sum(axis=-1))
            xj = cin_out
        cin_logits = jnp.concatenate(p_list, axis=1) @ cin_out_W + cin_out_b
        return linear_logits + dnn_logits + cin_logits

    y = _L0_rec_ref(r_dense_x, r_discrete_x, L0_rec_lin_emb, L0_rec_emb_W, L0_rec_dense_W, L0_rec_dense_b, L0_rec_W1, L0_rec_b1, L0_rec_bn1_g, L0_rec_bn1_b, L0_rec_W2, L0_rec_b2, L0_rec_bn2_g, L0_rec_bn2_b, L0_rec_W3, L0_rec_b3, L0_rec_bn3_g, L0_rec_bn3_b, L0_rec_Wout, L0_rec_bout, L0_rec_dense_proj, L0_rec_cin_W0, L0_rec_cin_W1, L0_rec_cin_W2, L0_rec_cin_out_W, L0_rec_cin_out_b)
    return y


_drawn_inputs = setup_inputs


def setup_inputs(seed=0):
    import zlib

    import numpy as np

    out = dict(_drawn_inputs(seed))
    spreads = {'L0_rec_b1': (0.0, 0.1),
     'L0_rec_bn1_g': (1.0, 0.2),
     'L0_rec_bn1_b': (0.0, 0.1),
     'L0_rec_b2': (0.0, 0.1),
     'L0_rec_bn2_g': (1.0, 0.2),
     'L0_rec_bn2_b': (0.0, 0.1),
     'L0_rec_b3': (0.0, 0.1),
     'L0_rec_bn3_g': (1.0, 0.2),
     'L0_rec_bn3_b': (0.0, 0.1)}
    factors = {'L0_rec_cin_W1': 7.566, 'L0_rec_cin_W2': 8.0}
    for name, (base, spread) in spreads.items():
        noise = np.random.default_rng([zlib.crc32(name.encode()), seed]).standard_normal(out[name].shape)
        drawn = base * np.exp(spread * noise) if base else spread * noise
        out[name] = jnp.asarray(drawn.astype(out[name].dtype))
    for name, factor in factors.items():
        out[name] = (out[name] * factor).astype(out[name].dtype)
    return out
```

```python
import concourse.bass as bass
from concourse import mybir
from contextlib import ExitStack
import math

P = 128
B = 1024
NS = 26
ND = 13
N = NS + ND
D = 16
V = 100000
F = 128
NT = B // P
NPAIR = NT // 2
DG = 4
NG = D // DG
CW = DG * P
NCH = 2 * NG
ROT = 21
RPT = 3
KT = ROT // RPT
KR = RPT * N
KQ = 2 * N
SLOT = N + 1
XR = 2 * SLOT + 1
EW = SLOT * D
DIN = NS * D + ND
H1, H2, H3 = 1024, 512, 256
K0, K1, K2, K3 = 4, H1 // P, H2 // P, H3 // P
KLAST = DIN - (K0 - 1) * P
PW = 2 * P
ROWS = [K1, K1, K1, K2, K2, K2, K3, K3, K3, 3, K3]
AT = [sum(ROWS[:i]) for i in range(len(ROWS) + 1)]
NPRM = AT[-1]
CW0, CW1, CW2, WO = AT[9], AT[9] + 1, AT[9] + 2, AT[10]
RSQ = 1.0 / math.sqrt(1.0 + 1e-5)
RING = 8
LAYER_AFTER = {3: 1, 4: 2, 5: 3}
TB = 12
SELW = (KT + 1) * KR


def build(nc, dense_x, discrete_x, lin_emb, emb_W, dense_W, dense_b, W1, b1, g1, be1, W2, b2, g2, be2,
          W3, b3, g3, be3, Wout, bout, dense_proj, cin_W0, cin_W1, cin_W2, cin_out_W, cin_out_b,
          consts, out):
    fp32 = mybir.dt.float32
    fr = mybir.dt.float32r
    i32 = mybir.dt.int32
    ALU = mybir.AluOpType
    ACT = mybir.ActivationFunctionType
    AX = mybir.AxisListType

    emb_rows = emb_W.rearrange("f v d -> (f v) d")
    lin_rows = lin_emb.rearrange("f v d -> (f v) d")

    with ExitStack() as ctx:
        def sb(name, shape, dt=fp32):
            return ctx.enter_context(nc.sbuf_tensor(name, shape, dt))

        def pb(name, shape, dt=fp32):
            return ctx.enter_context(nc.psum_tensor(name, shape, dt))

        def sem(name):
            return ctx.enter_context(nc.semaphore(name))

        ident = sb("ident", [P, P])
        sel = sb("sel", [XR, KT + 1, KR], fr)
        ones = sb("ones", [P, 1])
        prm = sb("prm", [P, NPRM])
        scale = sb("scale", [P, K1 + K2 + K3])
        shift = sb("shift", [P, K1 + K2 + K3])
        scalars = sb("scalars", [P, 3])
        bias = sb("bias", [P, 1])
        proj = sb("proj", [P, ND, D])
        dW = sb("dW", [P, ND])
        Vx = sb("Vx", [P, SLOT])
        AH = sb("AH", [KR, KT, P], fr)
        AL = sb("AL", [KR, KT, P], fr)
        BH = sb("BH", [KR, KT, P], fr)
        BL = sb("BL", [KR, KT, P], fr)
        W1H = sb("W1H", [P, K0, H1], fr)
        W1L = sb("W1L", [P, K0, H1], fr)
        W2H = sb("W2H", [P, K1, H2], fr)
        W2L = sb("W2L", [P, K1, H2], fr)
        W3H = sb("W3H", [P, K2, H3], fr)
        W3L = sb("W3L", [P, K2, H3], fr)
        idx = sb("idx", [P, NT, NS], i32)
        idx_emb = sb("idx_emb", [P, 2, NS], i32)
        idx_lin = sb("idx_lin", [P, 2, NS], i32)
        dns = sb("dns", [P, NT, ND])
        L = sb("L", [P, 2, NS])
        lin = sb("lin", [P, NPAIR, 2, NS])
        dlin = sb("dlin", [P, NT, ND])
        E = [sb(f"E{p}", [P, EW]) for p in range(2)]
        EE = [sb(f"EE{p}", [P, D, XR]) for p in range(2)]
        XT = [sb(f"XT{p}", [XR, CW], fr) for p in range(2)]
        X3 = [sb(f"X3{p}", [KR, CW]) for p in range(2)]
        Q = [sb(f"Q{s}", [KR, CW]) for s in range(4)]
        A0 = sb("A0", [P, K0, P])
        A0H = sb("A0H", [P, K0, PW], fr)
        A0L = sb("A0L", [P, K0, PW], fr)
        lsum = sb("lsum", [P, NT])
        dsum = sb("dsum", [P, NT])
        base = sb("base", [P, NT])
        res = sb("res", [P, NT])
        with ExitStack() as early:
            def eb(name, shape, dt=fp32):
                return early.enter_context(nc.sbuf_tensor(name, shape, dt))
            cst = eb("cst", [XR, SELW])
            prm_rows = eb("prm_rows", [NPRM, P])
            T = eb("T", [P, N, SLOT])
            sym = eb("sym", [P, N, 2 * N])
            rotw = eb("rotw", [P, ROT, N])
            w0raw = eb("w0raw", [P, N * N])
        QH = [sb(f"QH{s}", [KR, CW], fr) for s in range(RING)]
        QL = [sb(f"QL{s}", [KR, CW], fr) for s in range(RING)]
        with ExitStack() as early:
            raw = eb("raw", [P, 2 * F * N])
        w2raw, w1raw = raw[:, 0:F * N], raw[:, F * N:2 * F * N]
        at1, at2 = K0 * H1, K0 * H1 + K2 * H3
        d1raw, d3raw, d2raw = raw[:, 0:at1], raw[:, at1:at2], raw[:, at2:at2 + K1 * H2]
        x1 = sb("x1", [P, CW])
        A1 = sb("A1", [P, K1, PW])
        A1H = sb("A1H", [P, K1, PW], fr)
        A1L = sb("A1L", [P, K1, PW], fr)
        A2, A2H, A2L = A1[:, 0:K2, :], A1H[:, 0:K2, :], A1L[:, 0:K2, :]
        A3 = sb("A3", [P, K3, NPAIR, PW])
        red = sb("red", [P, NT, P])
        redc = sb("redc", [P, P])

        psS = [pb(f"psS{s}", [P, 512]) for s in range(2)]
        psR = [pb(f"psR{s}", [P, 512]) for s in range(2)]
        psA = [pb(f"psA{s}", [P, 512]) for s in range(2)]
        psB = [pb(f"psB{s}", [P, 512]) for s in range(2)]

        idx_in = sem("idx_in")
        w2_in = sem("w2_in")
        w1_in = sem("w1_in")
        w0_in = sem("w0_in")
        prm_in = sem("prm_in")
        cst_in = sem("cst_in")
        small_in = sem("small_in")
        d1_in = sem("d1_in")
        d2_in = sem("d2_in")
        d3_in = sem("d3_in")
        emb_in = [sem(f"emb_in{p}") for p in range(2)]
        lin_in = sem("lin_in")
        out_st = sem("out_st")
        pool_step = sem("pool_step")
        pool_go = sem("pool_go")
        lin_done = sem("lin_done")
        ones_set = sem("ones_set")
        prm_ps = sem("prm_ps")
        prm_sb = sem("prm_sb")
        aff = sem("aff")
        aff_done = sem("aff_done")
        v_ps = sem("v_ps")
        v_sb = sem("v_sb")
        t_ps = sem("t_ps")
        t_sb = sem("t_sb")
        sym_step = sem("sym_step")
        rotw_done = sem("rotw_done")
        rt_ps = sem("rt_ps")
        rt_hi = sem("rt_hi")
        rt_lo = sem("rt_lo")
        sel_done = sem("sel_done")
        wh_done = sem("wh_done")
        wl_done = sem("wl_done")
        prod_done = sem("prod_done")
        hi_done = sem("hi_done")
        lo_done = sem("lo_done")
        st_full = sem("st_full")
        st_free = sem("st_free")
        rot_full = sem("rot_full")
        mul_done = sem("mul_done")
        qh_done = sem("qh_done")
        ql_done = sem("ql_done")
        acc_done = sem("acc_done")
        x1_done = sem("x1_done")
        xy_done = sem("xy_done")
        red_done = sem("red_done")
        tot_done = sem("tot_done")
        act_h = sem("act_h")
        act_l = sem("act_l")
        fin_ps = sem("fin_ps")
        fin_sb = sem("fin_sb")

        block = ctx.enter_context(nc.Block())

        jobs = [("xt", 0), ("dn", 0), ("x3", 0), ("xt", 1), ("x3", 1)]
        before = len(jobs)
        for c in range(NCH):
            jobs += [("xt", c + 2)] + [("dn", (c + 2) // NG)] * (c + 2 in (NG, 2 * NG)) + [("x3", c + 2)]
            if c in LAYER_AFTER:
                jobs += [("out", LAYER_AFTER[c], m) for m in range((K1, K2, K3)[LAYER_AFTER[c] - 1])]
        job = {name: n for n, name in enumerate(jobs)}
        STP = len(jobs) - before
        assert STP % 2 == 0 and all(job[kind, n + m] == job[kind, n] + STP
                                    for kind, n, m in (("xt", 0, NCH), ("xt", 1, NCH), ("x3", 0, NCH), ("dn", 0, 2)))

        def emptied(i, *name):
            return STP * i + job[name] + 1

        @block.sync
        def _(sp):
            sp.dma_start(idx[:, :, :], discrete_x.rearrange("(p t) f -> p t f", t=NT)).then_inc(idx_in, 16)
            sp.dma_start(cst[:, :], consts[0:XR, 0:SELW]).then_inc(cst_in, 16)
            sp.dma_start(ident[:, :], consts[:, SELW:SELW + P]).then_inc(cst_in, 16)
            sp.dma_start(w2raw, cin_W2.rearrange("g f m -> g (f m)")).then_inc(w2_in, 16)
            sp.dma_start(w1raw, cin_W1.rearrange("f c n -> f (c n)")).then_inc(w1_in, 16)
            sp.wait_ge(v_ps, 1)
            sp.dma_start(d1raw[:, 0:(K0 - 1) * H1].rearrange("p (k n) -> p k n", n=H1),
                         W1[0:(K0 - 1) * P, :].rearrange("(k p) n -> p k n", p=P)).then_inc(d1_in, 16)
            sp.dma_start(d1raw[0:KLAST, (K0 - 1) * H1:K0 * H1], W1[(K0 - 1) * P:DIN, :]).then_inc(d1_in, 16)
            sp.wait_ge(t_ps, 1)
            sp.dma_start(d2raw.rearrange("p (k n) -> p k n", n=H2),
                         W2.rearrange("(k p) n -> p k n", p=P)).then_inc(d2_in, 16)
            sp.dma_start(d3raw.rearrange("p (k n) -> p k n", n=H3),
                         W3.rearrange("(k p) n -> p k n", p=P)).then_inc(d3_in, 16)
            sp.wait_ge(fin_sb, 1)
            sp.dma_start(out.rearrange("(p t) o -> p (t o)", t=NT), res[:, :]).then_inc(out_st, 16)
            sp.wait_ge(out_st, 16)

        @block.gpsimd
        def _(pool):
            def gather(dst, idx_col, rows, f, done):
                pool.indirect_dma_start(dst, None, rows, bass.IndirectOffsetOnAxis(ap=idx_col, axis=0),
                                        element_offset=f * V * rows.shape[1]).then_inc(done, 16)

            def gather_lin(dst):
                for p in range(2):
                    for f in range(NS):
                        gather(dst[:, p, f:f + 1], idx_lin[:, p, f:f + 1], lin_rows, f, lin_in)

            def gather_emb_next(i, copied):
                for p in range(2):
                    pool.wait_ge(emb_in[p], 16 * NS * i + 16 * NS)
                nc.gpsimd.tensor_copy(idx_emb[:, :, :], idx[:, bass.ds(2 * i + 2, 2), :]).then_inc(pool_step, 1)
                pool.wait_ge(pool_step, copied)
                for p in range(2):
                    pool.wait_ge(lo_done, 2 * i + p + 1)
                    pool.wait_ge(st_free, emptied(i, "dn", p))
                    pool.sem_inc(pool_go, 1)
                    for f in range(NS):
                        gather(E[p][:, f * D:(f + 1) * D], idx_emb[:, p, f:f + 1], emb_rows, f, emb_in[p])

            pool.wait_ge(idx_in, 16)
            nc.gpsimd.tensor_copy(idx_emb[:, :, :], idx[:, 0:2, :]).then_inc(pool_step, 1)
            nc.gpsimd.tensor_copy(idx_lin[:, :, :], idx[:, 0:2, :]).then_inc(pool_step, 1)
            pool.wait_ge(pool_step, 2)
            for p in range(2):
                for f in range(NS):
                    gather(E[p][:, f * D:(f + 1) * D], idx_emb[:, p, f:f + 1], emb_rows, f, emb_in[p])
            gather_emb_next(0, 3)
            gather_lin(L)
            with pool.Fori(1, NPAIR - 1) as i:
                gather_emb_next(i, 3 * i + 1)
                pool.wait_ge(lin_in, 2 * 16 * NS * i)
                nc.gpsimd.tensor_copy(lin[:, bass.ds(i - 1, 1), :, :].rearrange("p a t f -> p (a t) f"),
                                      L[:, :, :]).then_inc(pool_step, 1)
                nc.gpsimd.tensor_copy(idx_lin[:, :, :], idx[:, bass.ds(2 * i, 2), :]).then_inc(pool_step, 1)
                pool.wait_ge(pool_step, 3 * i + 3)
                pool.sem_inc(pool_go, 1)
                gather_lin(L)
            pool.wait_ge(lin_in, 2 * 16 * NS * (NPAIR - 1))
            nc.gpsimd.tensor_copy(lin[:, NPAIR - 2, :, :], L[:, :, :]).then_inc(lin_done, 1)
            nc.gpsimd.tensor_copy(idx_lin[:, :, :], idx[:, 2 * NPAIR - 2:2 * NPAIR, :]).then_inc(pool_step, 1)
            pool.wait_ge(pool_step, 3 * (NPAIR - 1) + 1)
            gather_lin(lin[:, NPAIR - 1, :, :])

        @block.tensor
        def _(pe):
            mm = nc.tensor.matmul
            pe.wait_ge(cst_in, 32)
            pe.wait_ge(prm_in, 16 * len(ROWS))
            nc.tensor.transpose(psS[0][:, 0:NPRM], prm_rows[:, :], ident[0:NPRM, 0:NPRM]).then_inc(prm_ps, 1)
            pe.wait_ge(prm_sb, 1)
            pe.wait_ge(w2_in, 16)
            w2v = w2raw.rearrange("g (f m) -> g m f", m=N)
            for m in range(N):
                last = mm(psS[1][:, m:m + 1], w2v[:, m, :], prm[:, CW2:CW2 + 1], start=True, stop=True)
            last.then_inc(v_ps, 1)
            pe.wait_ge(v_sb, 1)
            pe.wait_ge(w1_in, 16)
            w1v = w1raw.rearrange("f (c n) -> f n c", n=N)
            tb = [psA[0], psB[0], psA[1], psB[1]]
            for n in range(N):
                j = n % TB * SLOT
                last = mm(tb[n // TB][:, j:j + SLOT], w1v[:, n, :], Vx[:, :], start=True, stop=True)
            last.then_inc(t_ps, 1)

            def rotations(which):
                pe.wait_ge(rotw_done, which + 1)
                for k in range(KT):
                    r = which * KT + k
                    if r >= 2:
                        pe.wait_ge(rt_lo, r - 1)
                    nc.tensor.transpose(psR[r % 2][0:KR, 0:P],
                                        rotw[:, RPT * k:RPT * k + RPT, :].rearrange("c r i -> c (r i)"),
                                        ident[:, :]).then_inc(rt_ps, 1)

            rotations(0)
            rotations(1)

            def stage_bank(i, *name):
                n = job[name]
                if n >= 2:
                    pe.wait_ge(st_free, STP * i + n - 1)
                return psS[n % 2]

            def x_transpose(i, c):
                p, g = c // NG % 2, c % NG
                if g == 0:
                    pe.wait_ge(lo_done, 2 * i + c // NG + 1)
                ps = stage_bank(i, "xt", c)
                for d in range(DG):
                    last = nc.tensor.transpose(ps[0:XR, d * P:(d + 1) * P], EE[p][:, g * DG + d, :], ident[:, :])
                last.then_inc(st_full, 1)

            def dnn_transpose(i, t):
                ps = stage_bank(i, "dn", t)
                for k in range(K0):
                    last = nc.tensor.transpose(ps[:, k * P:(k + 1) * P], E[t % 2][:, k * P:(k + 1) * P], ident[:, :])
                last.then_inc(st_full, 1)

            def x_copies(i, c):
                pe.wait_ge(st_free, emptied(i, "xt", c))
                ps = stage_bank(i, "x3", c)
                mm(ps[0:KR, :], sel[:, KT, :], XT[c % 2][:, :], start=True, stop=True).then_inc(st_full, 1)

            def rotate(i, c, k):
                r = KT * c + k
                if k == 0:
                    pe.wait_ge(st_free, emptied(i, "xt", c))
                if r >= 2:
                    pe.wait_ge(mul_done, KT * NCH * i + r - 1)
                mm(psR[r % 2][0:KR, :], sel[:, k, :], XT[c % 2][:, :], start=True, stop=True).then_inc(rot_full, 1)

            def products(i, c, k):
                pe.wait_ge(ql_done, KT * (NCH * i + c) + k + 1)
                ka = KQ if k == KT - 1 else KR
                q = (KT * c + k) % RING
                h, l = QH[q][:, :], QL[q][:, :]
                first, lastk = k == 0, k == KT - 1
                mm(psA[c % 2][:, :], AH[0:ka, k, :], h[0:ka, :], start=first, stop=False)
                mm(psA[c % 2][:, :], AH[0:ka, k, :], l[0:ka, :], start=False, stop=False)
                mm(psA[c % 2][:, :], AL[0:ka, k, :], h[0:ka, :], start=False, stop=lastk)
                mm(psB[c % 2][:, :], BH[:, k, :], h, start=first, stop=False)
                mm(psB[c % 2][:, :], BH[:, k, :], l, start=False, stop=False)
                last = mm(psB[c % 2][:, :], BL[:, k, :], h, start=False, stop=lastk)
                if lastk:
                    last.then_inc(acc_done, 1)

            def layer(i, n):
                kk, mt = {1: (K0, K1), 2: (K1, K2), 3: (K2, K3)}[n]
                wh, wl, xh, xl = {1: (W1H, W1L, A0H, A0L), 2: (W2H, W2L, A1H, A1L), 3: (W3H, W3L, A2H, A2L)}[n]
                pe.wait_ge(wl_done, n)
                pe.wait_ge(act_l, 4 * i + n + 1)
                for m in range(mt):
                    ps = stage_bank(i, "out", n, m)
                    for k in range(kk):
                        rows = KLAST if n == 1 and k == K0 - 1 else P
                        w, v = wh[0:rows, k, m * P:(m + 1) * P], wl[0:rows, k, m * P:(m + 1) * P]
                        mm(ps[:, 0:PW], w, xh[0:rows, k, :], start=k == 0, stop=False)
                        mm(ps[:, 0:PW], w, xl[0:rows, k, :], start=False, stop=False)
                        last = mm(ps[:, 0:PW], v, xh[0:rows, k, :], start=False, stop=k == kk - 1)
                    last.then_inc(st_full, 1)

            pe.wait_ge(sel_done, 1)
            pe.wait_ge(rt_lo, 2 * KT)
            x_transpose(0, 0)
            dnn_transpose(0, 0)
            x_copies(0, 0)
            x_transpose(0, 1)
            x_copies(0, 1)
            for k in range(KT):
                rotate(0, 0, k)

            def pair(i, final):
                for c in range(NCH):
                    for k in range(KT):
                        if not (final and c + 1 == NCH):
                            rotate(i, c + 1, k)
                        products(i, c, k)
                        if k == 2 and not (final and c + 2 >= NCH):
                            x_transpose(i, c + 2)
                            if c + 2 == NG or c + 2 == 2 * NG:
                                dnn_transpose(i, (c + 2) // NG)
                        if k == 5 and not (final and c + 2 >= NCH):
                            x_copies(i, c + 2)
                    if c in LAYER_AFTER:
                        layer(i, LAYER_AFTER[c])

            with pe.Fori(0, NPAIR - 1) as i:
                pair(i, False)
            pair(NPAIR - 1, True)

            pe.wait_ge(tot_done, NT * (NG - 1))
            pe.wait_ge(st_free, emptied(NPAIR - 1, "out", 3, K3 - 1))
            ps = psR[0]
            for t in range(NT):
                mm(ps[:, t:t + 1], red[:, t, :], ones[:, :], start=True, stop=False)
                for k in range(K3):
                    last = mm(ps[:, t:t + 1], A3[:, k, t // 2, t % 2 * P:(t % 2 + 1) * P],
                              prm[:, WO + k:WO + k + 1], start=False, stop=k == K3 - 1)
            last.then_inc(fin_ps, 1)

        @block.scalar
        def _(act):
            rows = [b1, g1, be1, b2, g2, be2, b3, g3, be3]
            for j, src in enumerate(rows):
                act.dma_start(prm_rows[AT[j]:AT[j + 1], :], src.rearrange("(m p) -> m p", p=P)).then_inc(prm_in, 16)
            act.dma_start(prm_rows[CW0:CW0 + 3, :], cin_out_W.rearrange("(m p) o -> m (p o)", p=P)).then_inc(prm_in, 16)
            act.dma_start(prm_rows[WO:WO + K3, :], Wout.rearrange("(m p) o -> m (p o)", p=P)).then_inc(prm_in, 16)
            act.dma_start(w0raw[:, :], cin_W0.rearrange("f m n -> f (m n)")).then_inc(w0_in, 16)
            act.dma_start(dns[:, :, :], dense_x.rearrange("(p t) f -> p t f", t=NT)).then_inc(small_in, 16)
            act.dma_start(proj[:, :, :].rearrange("p j d -> p (j d)"),
                          dense_proj.rearrange("j d -> (j d)").partition_broadcast(P)).then_inc(small_in, 16)
            act.dma_start(dW[:, :], dense_W.rearrange("j o -> (j o)").partition_broadcast(P)).then_inc(small_in, 16)
            for j, src in enumerate((dense_b, bout, cin_out_b)):
                act.dma_start(scalars[:, j:j + 1], src.partition_broadcast(P)).then_inc(small_in, 16)

            copy = nc.scalar.copy
            act.wait_ge(cst_in, 32)
            copy(sel[:, :, :].rearrange("r k m -> r (k m)"), cst[:, :]).then_inc(sel_done, 1)
            act.wait_ge(prm_ps, 1)
            copy(prm[:, :], psS[0][:, 0:NPRM]).then_inc(prm_sb, 1)
            act.wait_ge(v_ps, 1)
            act.wait_ge(prm_sb, 1)
            copy(Vx[:, N:SLOT], prm[:, CW1:CW1 + 1])
            copy(Vx[:, 0:N], psS[1][:, 0:N]).then_inc(v_sb, 1)
            act.wait_ge(t_ps, 1)
            for j, ps in enumerate([psA[0], psB[0], psA[1], psB[1]]):
                n = min(TB, N - j * TB)
                last = copy(T[:, j * TB:j * TB + n, :].rearrange("c n m -> c (n m)"), ps[:, 0:n * SLOT])
            last.then_inc(t_sb, 1)
            for r in range(2 * KT):
                act.wait_ge(rt_ps, r + 1)
                copy((AH, BH)[r // KT][:, r % KT, :], psR[r % 2][0:KR, 0:P]).then_inc(rt_hi, 1)

            def full(i, *name):
                act.wait_ge(st_full, STP * i + job[name] + 1)
                return psS[job[name] % 2]

            def split_high(i, t):
                p = t % 2
                act.wait_ge(emb_in[p], 16 * NS * (i + t // 2 + 1))
                act.wait_ge(prod_done, 2 * i + t + 1)
                nc.scalar.copy(EE[p][:, :, 0:SLOT].bitcast(fr),
                               E[p][:, :].rearrange("b (n d) -> b d n", d=D)).then_inc(hi_done, 1)

            def round_high(i, c, k):
                r = KT * c + k
                act.wait_ge(mul_done, KT * NCH * i + r + 1)
                copy(QH[r % RING][:, :], Q[r % 4][:, :]).then_inc(qh_done, 1)

            def empty_xt(i, c):
                copy(XT[c % 2][:, :], full(i, "xt", c)[0:XR, :]).then_inc(st_free, 1)

            def empty_x3(i, c):
                copy(X3[c % 2][:, :], full(i, "x3", c)[0:KR, :]).then_inc(st_free, 1)

            def empty_dnn(i, t):
                ps = full(i, "dn", t)
                if t:
                    act.wait_ge(act_l, 4 * i + t)
                copy(A0[:, :, :].rearrange("a k b -> a (k b)"), ps[:, :]).then_inc(st_free, 1)

            def high_dnn_input(i, t):
                p = t % 2
                act.wait_ge(st_free, emptied(i, "dn", t))
                copy(A0H[:, :, p * P:(p + 1) * P], A0[:, :, :]).then_inc(act_h, 1)

            def relu(i, n):
                mt, off = {1: (K1, 0), 2: (K2, K1), 3: (K3, K1 + K2)}[n]
                for m in range(mt):
                    ps = full(i, "out", n, m)
                    dst = {1: lambda: A1[:, m, :], 2: lambda: A2[:, m, :],
                           3: lambda: A3[:, m, bass.ds(i, 1), :].rearrange("c a b -> c (a b)")}[n]()
                    nc.scalar.activation(dst, ps[:, 0:PW], ACT.Relu, bias=shift[:, off + m:off + m + 1],
                                                scale=scale[:, off + m:off + m + 1]).then_inc(st_free, 1)
                if n < 3:
                    act.wait_ge(st_free, emptied(i, "out", n, mt - 1))
                    src, dst = {1: (A1[:, :, :], A1H[:, :, :]), 2: (A2, A2H)}[n]
                    copy(dst, src).then_inc(act_h, 1)

            act.wait_ge(ones_set, 1)
            split_high(0, 0)
            empty_xt(0, 0)
            empty_dnn(0, 0)
            empty_x3(0, 0)
            empty_xt(0, 1)
            empty_x3(0, 1)
            high_dnn_input(0, 0)
            for k in range(KT):
                round_high(0, 0, k)
            act.wait_ge(d1_in, 32)
            copy(W1H[:, 0:K0 - 1, :].rearrange("p k n -> p (k n)"), d1raw[:, 0:(K0 - 1) * H1])
            copy(W1H[0:KLAST, K0 - 1, :], d1raw[0:KLAST, (K0 - 1) * H1:K0 * H1]).then_inc(wh_done, 1)
            act.wait_ge(d2_in, 16)
            copy(W2H[:, :, :].rearrange("p k n -> p (k n)"), d2raw).then_inc(wh_done, 1)
            act.wait_ge(d3_in, 16)
            copy(W3H[:, :, :].rearrange("p k n -> p (k n)"), d3raw).then_inc(wh_done, 1)
            act.wait_ge(aff_done, 1)
            act.wait_ge(wl_done, 3)

            def pair(i, final):
                for c in range(NCH):
                    if c + 3 in (NG, 2 * NG) and not (final and c + 3 == 2 * NG):
                        split_high(i, (c + 3) // NG)
                    for k in range(KT):
                        if not (final and c + 1 == NCH):
                            round_high(i, c + 1, k)
                        if k == 3 and not (final and c + 2 >= NCH):
                            empty_xt(i, c + 2)
                            if c + 2 in (NG, 2 * NG):
                                empty_dnn(i, (c + 2) // NG)
                        if k == 6 and not (final and c + 2 >= NCH):
                            empty_x3(i, c + 2)
                            if c + 2 in (NG, 2 * NG):
                                high_dnn_input(i, (c + 2) // NG)
                    act.wait_ge(acc_done, NCH * i + c + 1)
                    if final and c + 1 == NCH:
                        act.wait_ge(red_done, NCH * i + c)
                    copy(x1[:, :], psA[c % 2][:, :]).then_inc(x1_done, 1)
                    if c in LAYER_AFTER:
                        relu(i, LAYER_AFTER[c])

            with act.Fori(0, NPAIR - 1) as i:
                pair(i, False)
            pair(NPAIR - 1, True)

        @block.vector
        def _(dve):
            tt = nc.vector.tensor_tensor
            nc.vector.memset(ones[:, :], 1.0)
            for p in range(2):
                nc.vector.memset(E[p][:, DIN:SLOT * D - ND * D], 0.0)
                last = nc.vector.memset(EE[p][:, :, XR - 1:XR], 1.0)
            last.then_inc(ones_set, 1)

            def rotations(which, src):
                n = 4 * which
                for h in range(2):
                    last = tt(sym[:, :, h * N:(h + 1) * N], src, src.rearrange("c m n -> c n m"), ALU.add)
                last.then_inc(sym_step, 1)
                dve.wait_ge(sym_step, n + 1)
                if which:
                    dve.wait_ge(rt_ps, KT)
                flat = sym[:, :, :].rearrange("c m n -> c (m n)")
                for k in range(ROT - 1):
                    last = nc.vector.tensor_copy(rotw[:, k, :], flat[:, k:k + (2 * N + 1) * (N - 1) + 1:2 * N + 1])
                last.then_inc(sym_step, 1)
                if which:
                    nc.vector.tensor_copy(rotw[:, ROT - 1, :], T[:, :, N]).then_inc(sym_step, 1)
                else:
                    nc.vector.memset(rotw[:, ROT - 1, :], 0.0).then_inc(sym_step, 1)
                dve.wait_ge(sym_step, n + 3)
                nc.vector.tensor_scalar(rotw[:, 0, :], rotw[:, 0, :], 0.5, None, ALU.mult).then_inc(sym_step, 1)
                dve.wait_ge(sym_step, n + 4)
                nc.vector.tensor_copy(dlin[:, 0, 0:1], ones[:, :]).then_inc(rotw_done, 1)

            def low_weights(r0, r1):
                for r in range(r0, r1):
                    dve.wait_ge(rt_hi, r + 1)
                    lo, hi = ((AL, AH), (BL, BH))[r // KT]
                    tt(lo[:, r % KT, :], psR[r % 2][0:KR, 0:P], hi[:, r % KT, :].bitcast(fp32),
                       ALU.subtract).then_inc(rt_lo, 1)

            dve.wait_ge(w0_in, 16)
            rotations(0, w0raw[:, :].rearrange("c (m n) -> c m n", n=N))
            dve.wait_ge(prm_sb, 1)
            o = 0
            steps = 0
            for l, m in enumerate((K1, K2, K3)):
                nc.vector.tensor_scalar(scale[:, o:o + m], prm[:, AT[3 * l + 1]:AT[3 * l + 2]], RSQ, None,
                                        ALU.mult).then_inc(aff, 1)
                dve.wait_ge(aff, steps + 1)
                tt(shift[:, o:o + m], prm[:, AT[3 * l]:AT[3 * l + 1]], scale[:, o:o + m], ALU.mult).then_inc(aff, 1)
                dve.wait_ge(aff, steps + 2)
                tt(shift[:, o:o + m], shift[:, o:o + m], prm[:, AT[3 * l + 2]:AT[3 * l + 3]],
                   ALU.add).then_inc(aff, 1)
                steps += 3
                o += m
            dve.wait_ge(aff, steps)
            nc.vector.tensor_copy(dlin[:, 1, 0:1], ones[:, :]).then_inc(aff_done, 1)
            low_weights(0, KT)
            dve.wait_ge(t_sb, 1)
            rotations(1, T[:, :, 0:N])
            low_weights(KT, 2 * KT)

            def dense_parts(i, t):
                p = t % 2
                x = dns[:, bass.ds(2 * i + t, 1), :].rearrange("b a j -> b (a j)")
                nc.vector.tensor_copy(E[p][:, NS * D:DIN], x)
                tt(E[p][:, (NS + 1) * D:].rearrange("b (j d) -> b j d", d=D),
                   dns[:, bass.ds(2 * i + t, 1), :].rearrange("b a j -> b j a").broadcast_to([P, ND, D]),
                   proj[:, :, :], ALU.mult).then_inc(prod_done, 1)

            def split_low(i, t):
                p = t % 2
                dve.wait_ge(hi_done, 2 * i + t + 1)
                tt(EE[p][:, :, SLOT:2 * SLOT], E[p][:, :].rearrange("b (n d) -> b d n", d=D),
                   EE[p][:, :, 0:SLOT], ALU.subtract).then_inc(lo_done, 1)

            def multiply(i, c, k):
                r = KT * c + k
                if k == 0:
                    dve.wait_ge(st_free, emptied(i, "x3", c))
                if r >= 4:
                    dve.wait_ge(ql_done, KT * NCH * i + r - 3)
                dve.wait_ge(rot_full, KT * NCH * i + r + 1)
                tt(Q[r % 4][:, :], psR[r % 2][0:KR, :], X3[c % 2][:, :], ALU.mult).then_inc(mul_done, 1)

            def subtract(i, c, k):
                r = KT * c + k
                dve.wait_ge(qh_done, KT * NCH * i + r + 1)
                tt(QL[r % RING][:, :], Q[r % 4][:, :], QH[r % RING][:, :].bitcast(fp32),
                   ALU.subtract).then_inc(ql_done, 1)

            def chunk_products(i, c, between):
                for k in range(KT):
                    multiply(i, c, k)
                    if k:
                        subtract(i, c, k - 1)
                    between(k)
                subtract(i, c, KT - 1)

            def chunk_sum(i, c):
                dve.wait_ge(x1_done, NCH * i + c + 1)
                nc.vector.scalar_tensor_tensor(x1[:, :], psB[c % 2][:, :], prm[:, CW0:CW0 + 1], x1[:, :],
                                               ALU.add, ALU.mult).then_inc(xy_done, 1)
                dve.wait_ge(xy_done, NCH * i + c + 1)
                total = red[:, bass.ds(2 * i + c // NG, 1), :].rearrange("c a b -> c (a b)")
                part = total if c % NG == 0 else redc[:, :]
                nc.vector.tensor_reduce(part, x1[:, :].rearrange("c (d b) -> c b d", d=DG), AX.X,
                                        ALU.add).then_inc(red_done, 1)
                if c % NG:
                    dve.wait_ge(red_done, NCH * i + c + 1)
                    tt(total, total, redc[:, :], ALU.add).then_inc(tot_done, 1)

            def low_dnn_input(i, t):
                p = t % 2
                dve.wait_ge(act_h, 4 * i + t + 1 + (2 if t == 2 else 0))
                s = slice(p * P, (p + 1) * P)
                tt(A0L[:, :, s], A0[:, :, :], A0H[:, :, s].bitcast(fp32), ALU.subtract).then_inc(act_l, 1)

            def low_layer(i, n):
                dve.wait_ge(act_h, 4 * i + 2 + n)
                x, h, l = {1: (A1[:, :, :], A1H[:, :, :], A1L[:, :, :]), 2: (A2, A2H, A2L)}[n]
                tt(l, x, h.bitcast(fp32), ALU.subtract).then_inc(act_l, 1)

            dve.wait_ge(small_in, 6 * 16)
            dense_parts(0, 0)
            split_low(0, 0)
            chunk_products(0, 0, lambda k: low_dnn_input(0, 0) if k == 2 else None)
            dve.wait_ge(wh_done, 1)
            tt(W1L[:, 0:K0 - 1, :].rearrange("p k n -> p (k n)"), d1raw[:, 0:(K0 - 1) * H1],
               W1H[:, 0:K0 - 1, :].rearrange("p k n -> p (k n)").bitcast(fp32), ALU.subtract)
            tt(W1L[0:KLAST, K0 - 1, :], d1raw[0:KLAST, (K0 - 1) * H1:K0 * H1],
               W1H[0:KLAST, K0 - 1, :].bitcast(fp32), ALU.subtract).then_inc(wl_done, 1)
            dve.wait_ge(wh_done, 2)
            tt(W2L[:, :, :].rearrange("p k n -> p (k n)"), d2raw,
               W2H[:, :, :].rearrange("p k n -> p (k n)").bitcast(fp32), ALU.subtract).then_inc(wl_done, 1)
            dve.wait_ge(wh_done, 3)
            tt(W3L[:, :, :].rearrange("p k n -> p (k n)"), d3raw,
               W3H[:, :, :].rearrange("p k n -> p (k n)").bitcast(fp32), ALU.subtract).then_inc(wl_done, 1)

            def pair(i, final):
                for c in range(NCH):
                    t = (c + 3) // NG
                    if c + 3 in (NG, 2 * NG) and not (final and t == 2):
                        dense_parts(i, t)
                        split_low(i, t)
                    if not (final and c + 1 == NCH):
                        l = LAYER_AFTER.get(c - 1, 3)
                        chunk_products(i, c + 1, lambda k: low_layer(i, l) if k == 2 and l < 3 else None)
                    if c + 2 in (NG, 2 * NG) and not (final and c + 2 >= NCH):
                        low_dnn_input(i, (c + 2) // NG)
                    chunk_sum(i, c)

            with dve.Fori(0, NPAIR - 1) as i:
                pair(i, False)
            pair(NPAIR - 1, True)

            dve.wait_ge(lin_done, 1)
            dve.wait_ge(lin_in, 2 * 16 * NS * NPAIR)
            nc.vector.tensor_reduce(lsum[:, :], lin[:, :, :, :].rearrange("b q t f -> b (q t) f"), AX.X,
                                    ALU.add).then_inc(aff, 1)
            tt(dlin[:, :, :], dns[:, :, :], dW[:, :].rearrange("b (a j) -> b a j", a=1).broadcast_to([P, NT, ND]),
               ALU.mult).then_inc(aff, 1)
            nc.vector.tensor_reduce(bias[:, :], scalars[:, :], AX.X, ALU.add).then_inc(aff, 1)
            dve.wait_ge(aff, steps + 3)
            nc.vector.tensor_reduce(dsum[:, :], dlin[:, :, :], AX.X, ALU.add).then_inc(aff, 1)
            dve.wait_ge(aff, steps + 4)
            nc.vector.scalar_tensor_tensor(base[:, :], lsum[:, :], bias[:, 0:1], dsum[:, :], ALU.add,
                                           ALU.add).then_inc(aff, 1)
            dve.wait_ge(aff, steps + 5)
            dve.wait_ge(fin_ps, 1)
            tt(res[:, :], psR[0][:, 0:NT], base[:, :], ALU.add).then_inc(fin_sb, 1)


def _consts():
    import numpy as np
    c = np.zeros((P, SELW + P), np.float32)
    slot = [f if f < NS else f + 1 for f in range(N)]
    for k in range(KT + 1):
        for j in range(RPT):
            for i in range(N):
                col = k * KR + j * N + i
                rot = RPT * k + j
                if k < KT and rot == ROT - 1:
                    c[XR - 1, col] = 1.0
                    continue
                f = slot[(i + rot) % N] if k < KT else slot[i]
                c[f, col] = c[SLOT + f, col] = 1.0
    c[:, SELW:] = np.eye(P, dtype=np.float32)
    return c


_INS = ["r_dense_x", "r_discrete_x"] + ["L0_rec_" + n for n in (
    "lin_emb", "emb_W", "dense_W", "dense_b", "W1", "b1", "bn1_g", "bn1_b", "W2", "b2", "bn2_g", "bn2_b",
    "W3", "b3", "bn3_g", "bn3_b", "Wout", "bout", "dense_proj", "cin_W0", "cin_W1", "cin_W2",
    "cin_out_W", "cin_out_b")]


def kernel(**inputs):
    import numpy as _np
    import concourse.bacc as _bacc
    from concourse import mybir as _mybir
    from concourse.bass_utils import run_bass_kernel_spmd as _run

    nc = _bacc.Bacc("TRN2", target_bir_lowering=False, num_devices=1)
    arrays, args = {}, []
    for name in _INS + ["consts"]:
        a = _consts() if name == "consts" else _np.ascontiguousarray(inputs[name])
        arrays[f"in_{name}"] = a
        args.append(nc.dram_tensor(f"in_{name}", a.shape, _mybir.dt.from_np(a.dtype), kind="ExternalInput").ap())
    args.append(nc.dram_tensor("out_0", (B, 1), _mybir.dt.float32, kind="ExternalOutput").ap())
    build(nc, *args)
    r = _run(nc, [arrays], core_ids=[0])
    return r.results[0]["out_0"]
```

```python
import concourse.bass as bass
from concourse import mybir
from contextlib import ExitStack
import math

P = 128
B = 1024
NS = 26
ND = 13
N = NS + ND
D = 16
V = 100000
F = 128
NT = B // P
NPAIR = NT // 2
DG = 4
NG = D // DG
CW = DG * P
NCH = 2 * NG
ROT = 21
RPT = 3
KT = ROT // RPT
KR = RPT * N
KQ = 2 * N
SLOT = N + 1
XR = 2 * SLOT + 1
EW = SLOT * D
DIN = NS * D + ND
H1, H2, H3 = 1024, 512, 256
K0, K1, K2, K3 = 4, H1 // P, H2 // P, H3 // P
KLAST = DIN - (K0 - 1) * P
PW = 2 * P
ROWS = [K1, K1, K1, K2, K2, K2, K3, K3, K3, 3, K3]
AT = [sum(ROWS[:i]) for i in range(len(ROWS) + 1)]
NPRM = AT[-1]
CW0, CW1, CW2, WO = AT[9], AT[9] + 1, AT[9] + 2, AT[10]
RSQ = 1.0 / math.sqrt(1.0 + 1e-5)
RING = 8
NW = 96
PLAN = {(c, 2): ("xt", c + 2) for c in range(NCH)} | {(c, 5): ("x3", c + 2) for c in range(NCH)}
PLAN |= {(c, 3): ("dn", (c + 2) // NG) for c in (NG - 2, 2 * NG - 2)}
PLAN |= {(3, 0): ("out", 1, 0), (3, 3): ("out", 1, 1), (3, 4): ("out", 1, 2), (3, 6): ("out", 1, 3),
         (4, 0): ("out", 1, 4), (4, 3): ("out", 1, 5), (4, 4): ("out", 1, 6), (4, 6): ("out", 1, 7),
         (5, 6): ("out", 2, 0), (6, 0): ("out", 2, 1), (6, 4): ("out", 2, 2), (6, 6): ("out", 2, 3),
         (7, 4): ("out", 3, 0), (7, 6): ("out", 3, 1)}
SPLITS = {(4, 2): (1, 0, K1 // 2), (5, 1): (1, K1 // 2, K1 // 2), (7, 1): (2, 0, K2)}
SW = N + ROT - 2
TB = 11
SELW = (KT + 1) * KR


def build(nc, dense_x, discrete_x, lin_emb, emb_W, dense_W, dense_b, W1, b1, g1, be1, W2, b2, g2, be2,
          W3, b3, g3, be3, Wout, bout, dense_proj, cin_W0, cin_W1, cin_W2, cin_out_W, cin_out_b,
          consts, out):
    fp32 = mybir.dt.float32
    fr = mybir.dt.float32r
    i32 = mybir.dt.int32
    ALU = mybir.AluOpType
    ACT = mybir.ActivationFunctionType
    AX = mybir.AxisListType

    emb_rows = emb_W.rearrange("f v d -> (f v) d")
    lin_rows = lin_emb.rearrange("f v d -> (f v) d")

    with ExitStack() as ctx:
        def sb(name, shape, dt=fp32):
            return ctx.enter_context(nc.sbuf_tensor(name, shape, dt))

        def pb(name, shape, dt=fp32):
            return ctx.enter_context(nc.psum_tensor(name, shape, dt))

        def sem(name):
            return ctx.enter_context(nc.semaphore(name))

        ident = sb("ident", [P, P])
        identr = sb("identr", [P, P], fr)
        sel = sb("sel", [XR, KT + 1, KR], fr)
        ones = sb("ones", [P, 1])
        prm = sb("prm", [P, NPRM])
        scale = sb("scale", [P, K1 + K2 + K3])
        shift = sb("shift", [P, K1 + K2 + K3])
        scalars = sb("scalars", [P, 3])
        bias = sb("bias", [P, 1])
        proj = sb("proj", [P, ND, D])
        dW = sb("dW", [P, ND])
        Vx = sb("Vx", [P, NW])
        AH = sb("AH", [KR, KT, P], fr)
        AL = sb("AL", [KR, KT, P], fr)
        BH = sb("BH", [KR, KT, P], fr)
        BL = sb("BL", [KR, KT, P], fr)
        W1H = sb("W1H", [P, K0, H1], fr)
        W1L = sb("W1L", [P, K0, H1], fr)
        W2H = sb("W2H", [P, K1, H2], fr)
        W2L = sb("W2L", [P, K1, H2], fr)
        W3H = sb("W3H", [P, K2, H3], fr)
        W3L = sb("W3L", [P, K2, H3], fr)
        A0H = sb("A0H", [P, K0, PW], fr)
        A0L = sb("A0L", [P, K0, PW], fr)
        idx = sb("idx", [P, NT, NS], i32)
        idx_emb = sb("idx_emb", [P, 2, NS], i32)
        idx_lin = sb("idx_lin", [P, 2, NS], i32)
        dns = sb("dns", [P, NT, ND])
        L = sb("L", [P, 2, NS])
        lin = sb("lin", [P, NPAIR, 2, NS])
        dlin = sb("dlin", [P, NT, ND])
        E = [sb(f"E{p}", [P, EW]) for p in range(2)]
        EE = [sb(f"EE{p}", [P, D, XR], fr) for p in range(2)]
        XT = [sb(f"XT{p}", [XR, CW], fr) for p in range(2)]
        X3 = [sb(f"X3{p}", [KR, CW]) for p in range(2)]
        Q = [sb(f"Q{s}", [KR, CW]) for s in range(4)]
        A0 = sb("A0", [P, K0, P])
        lsum = sb("lsum", [P, NT])
        dsum = sb("dsum", [P, NT])
        base = sb("base", [P, NT])
        res = sb("res", [P, NT])
        with ExitStack() as early:
            def eb(name, shape, dt=fp32):
                return early.enter_context(nc.sbuf_tensor(name, shape, dt))
            cst = eb("cst", [XR, SELW])
            prm_rows = eb("prm_rows", [NPRM, P])
            T = eb("T", [P, N, SLOT])
            sym = eb("sym", [P, N * (SW + 1)])
            rotw = eb("rotw", [P, ROT, N])
            w0raw = eb("w0raw", [P, N * N])
            w2col = eb("w2col", [P, NW])
        QH = [sb(f"QH{s}", [KR, CW], fr) for s in range(RING)]
        QL = [sb(f"QL{s}", [KR, CW], fr) for s in range(RING)]
        with ExitStack() as early:
            raw = eb("raw", [P, 2 * F * N])
        w2raw, w1raw = raw[:, 0:F * N], raw[:, F * N:2 * F * N]
        at1, at2 = K0 * H1, K0 * H1 + K2 * H3
        d1raw, d3raw, d2raw = raw[:, 0:at1], raw[:, at1:at2], raw[:, at2:at2 + K1 * H2]
        x1 = sb("x1", [P, CW])
        A1 = sb("A1", [P, K1, PW])
        A1H = sb("A1H", [P, K1, PW], fr)
        A1L = sb("A1L", [P, K1, PW], fr)
        A2, A2H, A2L = A1[:, 0:K2, :], A1H[:, 0:K2, :], A1L[:, 0:K2, :]
        A3 = sb("A3", [P, K3, NPAIR, PW])
        red = sb("red", [P, NT, P])
        redc = sb("redc", [P, P])

        psS = [pb(f"psS{s}", [P, 512]) for s in range(2)]
        psR = [pb(f"psR{s}", [P, 512]) for s in range(2)]
        psA = [pb(f"psA{s}", [P, 512]) for s in range(2)]
        psB = [pb(f"psB{s}", [P, 512]) for s in range(2)]

        idx_in = sem("idx_in")
        w2_in = sem("w2_in")
        w1_in = sem("w1_in")
        w0_in = sem("w0_in")
        prm_in = sem("prm_in")
        cst_in = sem("cst_in")
        small_in = sem("small_in")
        d1_in = sem("d1_in")
        d2_in = sem("d2_in")
        d3_in = sem("d3_in")
        emb_in = [sem(f"emb_in{p}") for p in range(2)]
        lin_in = sem("lin_in")
        out_st = sem("out_st")
        pool_step = sem("pool_step")
        pool_go = sem("pool_go")
        lin_done = sem("lin_done")
        ones_set = sem("ones_set")
        prm_ps = sem("prm_ps")
        prm_sb = sem("prm_sb")
        aff = sem("aff")
        aff_done = sem("aff_done")
        w2_col = sem("w2_col")
        v_ps = sem("v_ps")
        v_sb = sem("v_sb")
        t_ps = sem("t_ps")
        t_sb = sem("t_sb")
        sym_step = sem("sym_step")
        rotw_done = sem("rotw_done")
        rt_ps = sem("rt_ps")
        rt_hi = sem("rt_hi")
        rt_lo = sem("rt_lo")
        sel_done = sem("sel_done")
        wh_done = sem("wh_done")
        wl_done = sem("wl_done")
        prod_done = sem("prod_done")
        hi_done = sem("hi_done")
        lo_done = sem("lo_done")
        st_full = sem("st_full")
        st_free = sem("st_free")
        rot_full = sem("rot_full")
        mul_done = sem("mul_done")
        qh_done = sem("qh_done")
        ql_done = sem("ql_done")
        acc_done = sem("acc_done")
        x1_done = sem("x1_done")
        xy_done = sem("xy_done")
        red_done = sem("red_done")
        tot_done = sem("tot_done")
        in_h = sem("in_h")
        in_l = sem("in_l")
        act_h = sem("act_h")
        act_l = sem("act_l")
        fin_ps = sem("fin_ps")
        fin_sb = sem("fin_sb")

        block = ctx.enter_context(nc.Block())

        jobs = [("xt", 0), ("dn", 0), ("x3", 0), ("xt", 1), ("x3", 1)]
        before = len(jobs)
        jobs += [PLAN[c, k] for c in range(NCH) for k in range(KT) if (c, k) in PLAN]
        job = {name: n for n, name in enumerate(jobs)}
        STP = len(jobs) - before
        last_jobs = [x for x in jobs if x[0] == "out" or x[1] < (NCH if x[0] != "dn" else 2)]
        last_job = {name: n for n, name in enumerate(last_jobs)}
        assert STP % 2 == 0
        assert all(job[kind, n + m] - STP <= job[kind, n]
                   for kind, n, m in (("xt", 0, NCH), ("xt", 1, NCH), ("x3", 0, NCH), ("x3", 1, NCH), ("dn", 0, 2)))

        def number(i, name):
            return (last_job if isinstance(i, int) and i == NPAIR - 1 else job)[name]

        def emptied(i, *name):
            return STP * i + number(i, name) + 1

        @block.sync
        def _(sp):
            sp.dma_start(idx[:, :, :], discrete_x.rearrange("(p t) f -> p t f", t=NT)).then_inc(idx_in, 16)
            sp.dma_start(ident[:, :], consts[:, SELW:SELW + P]).then_inc(cst_in, 16)
            sp.dma_start(w0raw[:, :], cin_W0.rearrange("f m n -> f (m n)")).then_inc(w0_in, 16)
            sp.dma_start(cst[:, :], consts[0:XR, 0:SELW]).then_inc(cst_in, 16)
            sp.dma_start(w2raw, cin_W2.rearrange("g f m -> g (f m)")).then_inc(w2_in, 16)
            sp.dma_start(w1raw, cin_W1.rearrange("f c n -> f (c n)")).then_inc(w1_in, 16)
            sp.dma_start(dns[:, :, :], dense_x.rearrange("(p t) f -> p t f", t=NT)).then_inc(small_in, 16)
            sp.dma_start(proj[:, :, :].rearrange("p j d -> p (j d)"),
                         dense_proj.rearrange("j d -> (j d)").partition_broadcast(P)).then_inc(small_in, 16)
            sp.dma_start(dW[:, :], dense_W.rearrange("j o -> (j o)").partition_broadcast(P)).then_inc(small_in, 16)
            for j, src in enumerate((dense_b, bout, cin_out_b)):
                sp.dma_start(scalars[:, j:j + 1], src.partition_broadcast(P)).then_inc(small_in, 16)
            sp.wait_ge(v_ps, 1)
            sp.dma_start(d1raw[:, 0:(K0 - 1) * H1].rearrange("p (k n) -> p k n", n=H1),
                         W1[0:(K0 - 1) * P, :].rearrange("(k p) n -> p k n", p=P)).then_inc(d1_in, 16)
            sp.dma_start(d1raw[0:KLAST, (K0 - 1) * H1:K0 * H1], W1[(K0 - 1) * P:DIN, :]).then_inc(d1_in, 16)
            sp.wait_ge(t_ps, 1)
            sp.dma_start(d2raw.rearrange("p (k n) -> p k n", n=H2),
                         W2.rearrange("(k p) n -> p k n", p=P)).then_inc(d2_in, 16)
            sp.dma_start(d3raw.rearrange("p (k n) -> p k n", n=H3),
                         W3.rearrange("(k p) n -> p k n", p=P)).then_inc(d3_in, 16)
            sp.wait_ge(fin_sb, 1)
            sp.dma_start(out.rearrange("(p t) o -> p (t o)", t=NT), res[:, :]).then_inc(out_st, 16)
            sp.wait_ge(out_st, 16)

        @block.gpsimd
        def _(pool):
            def gather(dst, idx_col, rows, f, done):
                pool.indirect_dma_start(dst, None, rows, bass.IndirectOffsetOnAxis(ap=idx_col, axis=0),
                                        element_offset=f * V * rows.shape[1]).then_inc(done, 16)

            def gather_lin(dst):
                for p in range(2):
                    for f in range(NS):
                        gather(dst[:, p, f:f + 1], idx_lin[:, p, f:f + 1], lin_rows, f, lin_in)

            def gather_emb_next(i, copied):
                for p in range(2):
                    pool.wait_ge(emb_in[p], 16 * NS * i + 16 * NS)
                nc.gpsimd.tensor_copy(idx_emb[:, :, :], idx[:, bass.ds(2 * i + 2, 2), :]).then_inc(pool_step, 1)
                pool.wait_ge(pool_step, copied)
                for p in range(2):
                    pool.wait_ge(lo_done, 2 * i + p + 1)
                    pool.wait_ge(st_free, emptied(i, "dn", p))
                    pool.sem_inc(pool_go, 1)
                    for f in range(NS):
                        gather(E[p][:, f * D:(f + 1) * D], idx_emb[:, p, f:f + 1], emb_rows, f, emb_in[p])

            pool.wait_ge(idx_in, 16)
            nc.gpsimd.tensor_copy(idx_emb[:, :, :], idx[:, 0:2, :]).then_inc(pool_step, 1)
            nc.gpsimd.tensor_copy(idx_lin[:, :, :], idx[:, 0:2, :]).then_inc(pool_step, 1)
            pool.wait_ge(pool_step, 2)
            for p in range(2):
                for f in range(NS):
                    gather(E[p][:, f * D:(f + 1) * D], idx_emb[:, p, f:f + 1], emb_rows, f, emb_in[p])
            gather_emb_next(0, 3)
            gather_lin(L)
            with pool.Fori(1, NPAIR - 1) as i:
                gather_emb_next(i, 3 * i + 1)
                pool.wait_ge(lin_in, 2 * 16 * NS * i)
                nc.gpsimd.tensor_copy(lin[:, bass.ds(i - 1, 1), :, :].rearrange("p a t f -> p (a t) f"),
                                      L[:, :, :]).then_inc(pool_step, 1)
                nc.gpsimd.tensor_copy(idx_lin[:, :, :], idx[:, bass.ds(2 * i, 2), :]).then_inc(pool_step, 1)
                pool.wait_ge(pool_step, 3 * i + 3)
                pool.sem_inc(pool_go, 1)
                gather_lin(L)
            pool.wait_ge(lin_in, 2 * 16 * NS * (NPAIR - 1))
            nc.gpsimd.tensor_copy(lin[:, NPAIR - 2, :, :], L[:, :, :]).then_inc(lin_done, 1)
            nc.gpsimd.tensor_copy(idx_lin[:, :, :], idx[:, 2 * NPAIR - 2:2 * NPAIR, :]).then_inc(pool_step, 1)
            pool.wait_ge(pool_step, 3 * (NPAIR - 1) + 1)
            gather_lin(lin[:, NPAIR - 1, :, :])

        @block.tensor
        def _(pe):
            mm = nc.tensor.matmul
            rt_banks = [psR[0], psR[1], psA[1], psB[1]]

            def rotations(which):
                pe.wait_ge(rotw_done, which + 1)
                for k in range(KT):
                    r = which * KT + k
                    if r >= 4:
                        pe.wait_ge(rt_lo, r - 3)
                    nc.tensor.transpose(rt_banks[r % 4][0:KR, 0:P],
                                        rotw[:, RPT * k:RPT * k + RPT, :].rearrange("c r i -> c (r i)"),
                                        ident[:, :]).then_inc(rt_ps, 1)

            pe.wait_ge(cst_in, 32)
            pe.wait_ge(prm_in, 16 * len(ROWS))
            nc.tensor.transpose(psS[0][:, 0:NPRM], prm_rows[:, :], ident[0:NPRM, 0:NPRM]).then_inc(prm_ps, 1)
            rotations(0)
            pe.wait_ge(w2_col, 1)
            pe.wait_ge(w2_in, 16)
            w2v = w2raw.rearrange("g (f m) -> g m f", m=N)
            for m in range(N):
                last = mm(psS[1][:, m:m + NW], w2v[:, m, :], w2col[:, :], start=True, stop=True)
            last.then_inc(v_ps, 1)
            pe.wait_ge(v_sb, 1)
            pe.wait_ge(rt_lo, KT)
            pe.wait_ge(w1_in, 16)
            w1v = w1raw.rearrange("f (c n) -> f n c", n=N)
            tb = [psA[0], psB[0], psA[1], psB[1]]
            for n in range(N):
                j = n % TB * SLOT
                last = mm(tb[n // TB][:, j:j + NW], w1v[:, n, :], Vx[:, :], start=True, stop=True)
            last.then_inc(t_ps, 1)

            def stage_bank(i, *name):
                n = number(i, name)
                if n >= 2:
                    pe.wait_ge(st_free, STP * i + n - 1)
                return psS[n % 2]

            def x_transpose(i, c):
                p, g = c // NG % 2, c % NG
                if g == 0:
                    pe.wait_ge(lo_done, 2 * i + c // NG + 1)
                ps = stage_bank(i, "xt", c)
                for d in range(DG):
                    last = mm(ps[0:XR, d * P:(d + 1) * P], EE[p][:, g * DG + d, :], identr[:, :],
                              start=True, stop=True)
                last.then_inc(st_full, 1)

            def dnn_transpose(i, t):
                ps = stage_bank(i, "dn", t)
                for k in range(K0):
                    last = nc.tensor.transpose(ps[:, k * P:(k + 1) * P], E[t % 2][:, k * P:(k + 1) * P], ident[:, :])
                last.then_inc(st_full, 1)

            def x_copies(i, c):
                pe.wait_ge(st_free, emptied(i, "xt", c))
                ps = stage_bank(i, "x3", c)
                mm(ps[0:KR, :], sel[:, KT, :], XT[c % 2][:, :], start=True, stop=True).then_inc(st_full, 1)

            def rotate(i, c, k):
                r = KT * c + k
                if k == 0:
                    pe.wait_ge(st_free, emptied(i, "xt", c))
                if r >= 2:
                    pe.wait_ge(mul_done, KT * NCH * i + r - 1)
                mm(psR[r % 2][0:KR, :], sel[:, k, :], XT[c % 2][:, :], start=True, stop=True).then_inc(rot_full, 1)

            def products(i, c, k):
                pe.wait_ge(ql_done, KT * (NCH * i + c) + k + 1)
                ka = KQ if k == KT - 1 else KR
                q = (KT * c + k) % RING
                h, l = QH[q][:, :], QL[q][:, :]
                first, lastk = k == 0, k == KT - 1
                mm(psA[c % 2][:, :], AH[0:ka, k, :], h[0:ka, :], start=first, stop=False)
                mm(psA[c % 2][:, :], AH[0:ka, k, :], l[0:ka, :], start=False, stop=False)
                mm(psA[c % 2][:, :], AL[0:ka, k, :], h[0:ka, :], start=False, stop=lastk)
                mm(psB[c % 2][:, :], BH[:, k, :], h, start=first, stop=False)
                mm(psB[c % 2][:, :], BH[:, k, :], l, start=False, stop=False)
                last = mm(psB[c % 2][:, :], BL[:, k, :], h, start=False, stop=lastk)
                if lastk:
                    last.then_inc(acc_done, 1)

            def outputs(i, n, m):
                kk = (K0, K1, K2)[n - 1]
                wh, wl, xh, xl = {1: (W1H, W1L, A0H, A0L), 2: (W2H, W2L, A1H, A1L), 3: (W3H, W3L, A2H, A2L)}[n]
                if m == 0:
                    pe.wait_ge(wl_done, n)
                    if n == 1:
                        pe.wait_ge(in_l, 2 * i + 2)
                    else:
                        pe.wait_ge(act_l, 3 * i + n)
                ps = stage_bank(i, "out", n, m)
                for k in range(kk):
                    rows = KLAST if n == 1 and k == K0 - 1 else P
                    w, v = wh[0:rows, k, m * P:(m + 1) * P], wl[0:rows, k, m * P:(m + 1) * P]
                    mm(ps[:, 0:PW], w, xh[0:rows, k, :], start=k == 0, stop=False)
                    mm(ps[:, 0:PW], w, xl[0:rows, k, :], start=False, stop=False)
                    last = mm(ps[:, 0:PW], v, xh[0:rows, k, :], start=False, stop=k == kk - 1)
                last.then_inc(st_full, 1)

            pe.wait_ge(sel_done, 2)
            x_transpose(0, 0)
            dnn_transpose(0, 0)
            x_copies(0, 0)
            x_transpose(0, 1)
            x_copies(0, 1)
            rotations(1)
            pe.wait_ge(rt_lo, 2 * KT)
            for k in range(KT):
                rotate(0, 0, k)

            run = {"xt": x_transpose, "dn": dnn_transpose, "x3": x_copies, "out": outputs}

            def pair(i, final):
                for c in range(NCH):
                    for k in range(KT):
                        if not (final and c + 1 == NCH):
                            rotate(i, c + 1, k)
                        products(i, c, k)
                        what, *which = PLAN.get((c, k), (None,))
                        if what == "out" or what and not (final and c + 2 >= NCH):
                            run[what](i, *which)
                        if final and c + 1 == NCH and k < NT - 2:
                            if k == 0:
                                pe.wait_ge(mul_done, KT * NT * NG)
                            logits(psR[0], k).then_inc(fin_ps, 1)

            def logits(bank, t):
                for k in range(K3):
                    mm(bank[:, t:t + 1], A3[:, k, t // 2, t % 2 * P:(t % 2 + 1) * P],
                       prm[:, WO + k:WO + k + 1], start=k == 0, stop=False)
                pe.wait_ge(tot_done, (t + 1) * (NG - 1))
                return mm(bank[:, t:t + 1], red[:, t, :], ones[:, :], start=False, stop=True)

            with pe.Fori(0, NPAIR - 1) as i:
                pair(i, False)
            pair(NPAIR - 1, True)
            pe.wait_ge(st_free, emptied(NPAIR - 1, "out", 3, K3 - 1))
            for t in (NT - 2, NT - 1):
                logits(psR[1], t).then_inc(fin_ps, 1)

        @block.scalar
        def _(act):
            act.dma_start(prm_rows[CW0:CW0 + 3, :], cin_out_W.rearrange("(m p) o -> m (p o)", p=P)).then_inc(prm_in, 16)
            rows = [b1, g1, be1, b2, g2, be2, b3, g3, be3]
            for j, src in enumerate(rows):
                act.dma_start(prm_rows[AT[j]:AT[j + 1], :], src.rearrange("(m p) -> m p", p=P)).then_inc(prm_in, 16)
            act.dma_start(prm_rows[WO:WO + K3, :], Wout.rearrange("(m p) o -> m (p o)", p=P)).then_inc(prm_in, 16)
            copy = nc.scalar.copy
            act.wait_ge(cst_in, 32)
            copy(identr[:, :], ident[:, :]).then_inc(sel_done, 1)
            copy(sel[:, :, :].rearrange("r k m -> r (k m)"), cst[:, :]).then_inc(sel_done, 1)
            act.wait_ge(prm_ps, 1)
            copy(prm[:, :], psS[0][:, 0:NPRM]).then_inc(prm_sb, 1)
            rt_banks = [psR[0], psR[1], psA[1], psB[1]]

            def high_rotations(which):
                for r in range(which * KT, (which + 1) * KT):
                    act.wait_ge(rt_ps, r + 1)
                    copy((AH, BH)[which][:, r % KT, :], rt_banks[r % 4][0:KR, 0:P]).then_inc(rt_hi, 1)

            act.wait_ge(prm_sb, 1)
            act.wait_ge(ones_set, 1)
            copy(w2col[:, 0:1], prm[:, CW2:CW2 + 1]).then_inc(w2_col, 1)
            high_rotations(0)
            act.wait_ge(v_ps, 1)
            copy(Vx[:, N:SLOT], prm[:, CW1:CW1 + 1])
            copy(Vx[:, 0:N], psS[1][:, 0:N]).then_inc(v_sb, 1)
            act.wait_ge(t_ps, 1)
            for j, ps in enumerate([psA[0], psB[0], psA[1], psB[1]]):
                n = min(TB, N - j * TB)
                last = copy(T[:, j * TB:j * TB + n, :].rearrange("c n m -> c (n m)"), ps[:, 0:n * SLOT])
            last.then_inc(t_sb, 1)
            act.wait_ge(d1_in, 32)
            copy(W1H[:, 0:K0 - 1, :].rearrange("p k n -> p (k n)"), d1raw[:, 0:(K0 - 1) * H1])
            copy(W1H[0:KLAST, K0 - 1, :], d1raw[0:KLAST, (K0 - 1) * H1:K0 * H1]).then_inc(wh_done, 1)

            def full(i, *name):
                n = number(i, name)
                act.wait_ge(st_full, STP * i + n + 1)
                return psS[n % 2]

            def split_high(i, t):
                p = t % 2
                act.wait_ge(emb_in[p], 16 * NS * (i + t // 2 + 1))
                act.wait_ge(prod_done, 2 * i + t + 1)
                nc.scalar.copy(EE[p][:, :, 0:SLOT],
                               E[p][:, :].rearrange("b (n d) -> b d n", d=D)).then_inc(hi_done, 1)

            def round_high(i, c, k):
                r = KT * c + k
                act.wait_ge(mul_done, KT * NCH * i + r + 1)
                copy(QH[r % RING][:, :], Q[r % 4][:, :]).then_inc(qh_done, 1)

            def empty_xt(i, c):
                copy(XT[c % 2][:, :], full(i, "xt", c)[0:XR, :]).then_inc(st_free, 1)

            def empty_x3(i, c):
                copy(X3[c % 2][:, :], full(i, "x3", c)[0:KR, :]).then_inc(st_free, 1)

            def empty_dnn(i, t):
                ps = full(i, "dn", t)
                if t:
                    act.wait_ge(in_l, 2 * i + t)
                copy(A0[:, :, :].rearrange("a k b -> a (k b)"), ps[:, :]).then_inc(st_free, 1)

            def high_dnn_input(i, t):
                p = t % 2
                act.wait_ge(st_free, emptied(i, "dn", t))
                copy(A0H[:, :, p * P:(p + 1) * P], A0[:, :, :]).then_inc(in_h, 1)

            def relu(i, n, m):
                o = (0, K1, K1 + K2)[n - 1] + m
                if n == 3:
                    dst = A3[:, m, bass.ds(i, 1), :].rearrange("c a b -> c (a b)")
                else:
                    dst = (A1, A2)[n - 1][:, m, :]
                nc.scalar.activation(dst, full(i, "out", n, m)[:, 0:PW], ACT.Relu, bias=shift[:, o:o + 1],
                                     scale=scale[:, o:o + 1]).then_inc(st_free, 1)

            def high_activations(i, n, m0, mt):
                act.wait_ge(st_free, emptied(i, "out", n, m0 + mt - 1))
                src, dst = ((A1, A1H), (A2, A2H))[n - 1]
                copy(dst[:, m0:m0 + mt, :], src[:, m0:m0 + mt, :]).then_inc(act_h, 1)

            run = {"xt": empty_xt, "dn": empty_dnn, "x3": empty_x3, "out": relu}

            act.wait_ge(ones_set, 2)
            split_high(0, 0)
            empty_xt(0, 0)
            empty_dnn(0, 0)
            empty_x3(0, 0)
            empty_xt(0, 1)
            empty_x3(0, 1)
            high_rotations(1)
            for k in range(KT):
                round_high(0, 0, k)
                if k == 2:
                    high_dnn_input(0, 0)
            act.wait_ge(d2_in, 16)
            copy(W2H[:, :, :].rearrange("p k n -> p (k n)"), d2raw).then_inc(wh_done, 1)
            act.wait_ge(d3_in, 16)
            copy(W3H[:, :, :].rearrange("p k n -> p (k n)"), d3raw).then_inc(wh_done, 1)
            act.wait_ge(aff_done, 1)
            act.wait_ge(wl_done, 3)

            def pair(i, final):
                def empty(c, k):
                    what, *which = PLAN.get((c, k), (None,))
                    if what == "out" or what and not (final and c + 2 >= NCH):
                        run[what](i, *which)

                for c in range(NCH):
                    for k in range(KT):
                        if not (final and c + 1 == NCH):
                            round_high(i, c + 1, k)
                        if k == 1 and c + 3 in (NG, 2 * NG) and not (final and c + 3 == 2 * NG):
                            split_high(i, (c + 3) // NG)
                        if k:
                            empty(c, k - 1)
                        if (c, k) in SPLITS:
                            high_activations(i, *SPLITS[c, k])
                        if k == 5 and PLAN.get((c, 3), ("",))[0] == "dn" and not (final and c + 2 >= NCH):
                            high_dnn_input(i, (c + 2) // NG)
                    act.wait_ge(acc_done, NCH * i + c + 1)
                    if final and c + 1 == NCH:
                        act.wait_ge(red_done, NCH * i + c)
                    copy(x1[:, :], psA[c % 2][:, :]).then_inc(x1_done, 1)
                    empty(c, KT - 1)

            with act.Fori(0, NPAIR - 1) as i:
                pair(i, False)
            pair(NPAIR - 1, True)

        @block.vector
        def _(dve):
            tt = nc.vector.tensor_tensor
            nc.vector.memset(w2col[:, :], 0.0)
            nc.vector.memset(Vx[:, :], 0.0)
            nc.vector.memset(ones[:, :], 1.0).then_inc(ones_set, 1)
            dve.wait_ge(ones_set, 1)
            for p in range(2):
                nc.vector.memset(E[p][:, DIN:SLOT * D - ND * D], 0.0)
                last = nc.vector.tensor_copy(EE[p][:, :, XR - 1:XR], ones[:, :].rearrange("p (a b) -> p a b", a=1).broadcast_to([P, D, 1]))
            last.then_inc(ones_set, 1)

            def rotations(which, src):
                n = 2 * which
                if which:
                    dve.wait_ge(rt_ps, KT)
                view = sym[:, 0:N * SW].rearrange("c (m n) -> c m n", n=SW)
                turned = src.rearrange("c m n -> c n m")
                tt(view[:, :, 0:N], src, turned, ALU.add)
                tt(view[:, :, N:SW], src[:, :, 0:SW - N], turned[:, :, 0:SW - N], ALU.add).then_inc(sym_step, 1)
                dve.wait_ge(sym_step, n + 1)
                nc.vector.tensor_copy(rotw[:, 0:ROT - 1, :],
                                      sym[:, :].rearrange("c (i j) -> c j i", j=SW + 1)[:, 0:ROT - 1, :])
                if which:
                    last = nc.vector.tensor_copy(rotw[:, ROT - 1, :], T[:, :, N])
                else:
                    last = nc.vector.memset(rotw[:, ROT - 1, :], 0.0)
                last.then_inc(sym_step, 1)
                dve.wait_ge(sym_step, n + 2)
                nc.vector.tensor_scalar(rotw[:, 0, :], rotw[:, 0, :], 0.5, None, ALU.mult).then_inc(rotw_done, 1)

            rt_banks = [psR[0], psR[1], psA[1], psB[1]]

            def low_rotations(which):
                lo, hi = ((AL, AH), (BL, BH))[which]
                for r in range(which * KT, (which + 1) * KT):
                    dve.wait_ge(rt_hi, r + 1)
                    tt(lo[:, r % KT, :], rt_banks[r % 4][0:KR, 0:P], hi[:, r % KT, :].bitcast(fp32),
                       ALU.subtract).then_inc(rt_lo, 1)

            dve.wait_ge(w0_in, 16)
            rotations(0, w0raw[:, :].rearrange("c (m n) -> c m n", n=N))
            low_rotations(0)
            dve.wait_ge(prm_sb, 1)
            o = 0
            steps = 0
            for l, m in enumerate((K1, K2, K3)):
                nc.vector.tensor_scalar(scale[:, o:o + m], prm[:, AT[3 * l + 1]:AT[3 * l + 2]], RSQ, None,
                                        ALU.mult).then_inc(aff, 1)
                dve.wait_ge(aff, steps + 1)
                tt(shift[:, o:o + m], prm[:, AT[3 * l]:AT[3 * l + 1]], scale[:, o:o + m], ALU.mult).then_inc(aff, 1)
                dve.wait_ge(aff, steps + 2)
                last = tt(shift[:, o:o + m], shift[:, o:o + m], prm[:, AT[3 * l + 2]:AT[3 * l + 3]], ALU.add)
                last.then_inc(aff_done if l == 2 else aff, 1)
                steps += 3 if l < 2 else 2
                o += m

            def dense_parts(i, t):
                p = t % 2
                x = dns[:, bass.ds(2 * i + t, 1), :].rearrange("b a j -> b (a j)")
                nc.vector.tensor_copy(E[p][:, NS * D:DIN], x)
                tt(E[p][:, (NS + 1) * D:].rearrange("b (j d) -> b j d", d=D),
                   dns[:, bass.ds(2 * i + t, 1), :].rearrange("b a j -> b j a").broadcast_to([P, ND, D]),
                   proj[:, :, :], ALU.mult).then_inc(prod_done, 1)

            def split_low(i, t):
                p = t % 2
                dve.wait_ge(hi_done, 2 * i + t + 1)
                tt(EE[p][:, :, SLOT:2 * SLOT], E[p][:, :].rearrange("b (n d) -> b d n", d=D),
                   EE[p][:, :, 0:SLOT].bitcast(fp32), ALU.subtract).then_inc(lo_done, 1)

            def multiply(i, c, k):
                r = KT * c + k
                if k == 0:
                    dve.wait_ge(st_free, emptied(i, "x3", c))
                if r >= 4:
                    dve.wait_ge(ql_done, KT * NCH * i + r - 3)
                dve.wait_ge(rot_full, KT * NCH * i + r + 1)
                tt(Q[r % 4][:, :], psR[r % 2][0:KR, :], X3[c % 2][:, :], ALU.mult).then_inc(mul_done, 1)

            def subtract(i, c, k):
                r = KT * c + k
                dve.wait_ge(qh_done, KT * NCH * i + r + 1)
                tt(QL[r % RING][:, :], Q[r % 4][:, :], QH[r % RING][:, :].bitcast(fp32),
                   ALU.subtract).then_inc(ql_done, 1)

            def chunk_products(i, c, between, begun=False):
                for k in range(KT):
                    if k or not begun:
                        multiply(i, c, k)
                    if k:
                        subtract(i, c, k - 1)
                    between(k)
                subtract(i, c, KT - 1)

            def chunk_sum(i, c):
                dve.wait_ge(x1_done, NCH * i + c + 1)
                nc.vector.scalar_tensor_tensor(x1[:, :], psB[c % 2][:, :], prm[:, CW0:CW0 + 1], x1[:, :],
                                               ALU.add, ALU.mult).then_inc(xy_done, 1)
                dve.wait_ge(xy_done, NCH * i + c + 1)
                total = red[:, bass.ds(2 * i + c // NG, 1), :].rearrange("c a b -> c (a b)")
                part = total if c % NG == 0 else redc[:, :]
                nc.vector.tensor_reduce(part, x1[:, :].rearrange("c (d b) -> c b d", d=DG), AX.X,
                                        ALU.add).then_inc(red_done, 1)
                if c % NG:
                    dve.wait_ge(red_done, NCH * i + c + 1)
                    tt(total, total, redc[:, :], ALU.add).then_inc(tot_done, 1)

            def low_dnn_input(i, t):
                dve.wait_ge(in_h, 2 * i + t + 1)
                s = slice(t % 2 * P, (t % 2 + 1) * P)
                tt(A0L[:, :, s], A0[:, :, :], A0H[:, :, s].bitcast(fp32), ALU.subtract).then_inc(in_l, 1)

            def low_activations(i, piece, n, m0, mt):
                dve.wait_ge(act_h, 3 * i + piece + 1)
                x, h, l = ((A1, A1H, A1L), (A2, A2H, A2L))[n - 1]
                tt(l[:, m0:m0 + mt, :], x[:, m0:m0 + mt, :], h[:, m0:m0 + mt, :].bitcast(fp32),
                   ALU.subtract).then_inc(act_l, 1)

            dve.wait_ge(small_in, 6 * 16)
            dense_parts(0, 0)
            split_low(0, 0)
            dve.wait_ge(t_sb, 1)
            rotations(1, T[:, :, 0:N])
            low_rotations(1)
            dve.wait_ge(wh_done, 1)
            tt(W1L[:, 0:K0 - 1, :].rearrange("p k n -> p (k n)"), d1raw[:, 0:(K0 - 1) * H1],
               W1H[:, 0:K0 - 1, :].rearrange("p k n -> p (k n)").bitcast(fp32), ALU.subtract)
            tt(W1L[0:KLAST, K0 - 1, :], d1raw[0:KLAST, (K0 - 1) * H1:K0 * H1],
               W1H[0:KLAST, K0 - 1, :].bitcast(fp32), ALU.subtract).then_inc(wl_done, 1)
            chunk_products(0, 0, lambda k: low_dnn_input(0, 0) if k == 3 else None)
            dve.wait_ge(wh_done, 2)
            tt(W2L[:, :, :].rearrange("p k n -> p (k n)"), d2raw,
               W2H[:, :, :].rearrange("p k n -> p (k n)").bitcast(fp32), ALU.subtract).then_inc(wl_done, 1)
            dve.wait_ge(wh_done, 3)
            tt(W3L[:, :, :].rearrange("p k n -> p (k n)"), d3raw,
               W3H[:, :, :].rearrange("p k n -> p (k n)").bitcast(fp32), ALU.subtract).then_inc(wl_done, 1)

            def pair(i, final):
                for c in range(NCH):
                    t = (c + 3) // NG

                    def between(k):
                        if c + 3 in (NG, 2 * NG) and not (final and t == 2):
                            if k == 0:
                                dense_parts(i, t)
                            if k == 2:
                                split_low(i, t)
                        if (c, k) in SPLITS:
                            low_activations(i, list(SPLITS).index((c, k)), *SPLITS[c, k])
                        if k == 6 and PLAN.get((c, 3), ("",))[0] == "dn" and not (final and c + 2 >= NCH):
                            low_dnn_input(i, (c + 2) // NG)

                    if final and c + 1 == NCH:
                        for k in range(KT):
                            between(k)
                    else:
                        chunk_products(i, c + 1, between, begun=True)
                    if not (final and c + 2 >= NCH):
                        multiply(i, c + 2, 0)
                    chunk_sum(i, c)

            multiply(0, 1, 0)
            with dve.Fori(0, NPAIR - 1) as i:
                pair(i, False)
            pair(NPAIR - 1, True)

            dve.wait_ge(lin_done, 1)
            dve.wait_ge(lin_in, 2 * 16 * NS * NPAIR)
            nc.vector.tensor_reduce(lsum[:, :], lin[:, :, :, :].rearrange("b q t f -> b (q t) f"), AX.X,
                                    ALU.add).then_inc(aff, 1)
            tt(dlin[:, :, :], dns[:, :, :], dW[:, :].rearrange("b (a j) -> b a j", a=1).broadcast_to([P, NT, ND]),
               ALU.mult).then_inc(aff, 1)
            nc.vector.tensor_reduce(bias[:, :], scalars[:, :], AX.X, ALU.add).then_inc(aff, 1)
            dve.wait_ge(aff, steps + 3)
            nc.vector.tensor_reduce(dsum[:, :], dlin[:, :, :], AX.X, ALU.add).then_inc(aff, 1)
            dve.wait_ge(aff, steps + 4)
            nc.vector.scalar_tensor_tensor(base[:, :], lsum[:, :], bias[:, 0:1], dsum[:, :], ALU.add,
                                           ALU.add).then_inc(aff, 1)
            dve.wait_ge(aff, steps + 5)
            dve.wait_ge(fin_ps, NT - 2)
            tt(res[:, 0:NT - 2], psR[0][:, 0:NT - 2], base[:, 0:NT - 2], ALU.add)
            dve.wait_ge(fin_ps, NT)
            tt(res[:, NT - 2:NT], psR[1][:, NT - 2:NT], base[:, NT - 2:NT], ALU.add).then_inc(fin_sb, 1)


def _consts():
    import numpy as np
    c = np.zeros((P, SELW + P), np.float32)
    slot = [f if f < NS else f + 1 for f in range(N)]
    for k in range(KT + 1):
        for j in range(RPT):
            for i in range(N):
                col = k * KR + j * N + i
                rot = RPT * k + j
                if k < KT and rot == ROT - 1:
                    c[XR - 1, col] = 1.0
                    continue
                f = slot[(i + rot) % N] if k < KT else slot[i]
                c[f, col] = c[SLOT + f, col] = 1.0
    c[:, SELW:] = np.eye(P, dtype=np.float32)
    return c


_INS = ["r_dense_x", "r_discrete_x"] + ["L0_rec_" + n for n in (
    "lin_emb", "emb_W", "dense_W", "dense_b", "W1", "b1", "bn1_g", "bn1_b", "W2", "b2", "bn2_g", "bn2_b",
    "W3", "b3", "bn3_g", "bn3_b", "Wout", "bout", "dense_proj", "cin_W0", "cin_W1", "cin_W2",
    "cin_out_W", "cin_out_b")]


def kernel(**inputs):
    import numpy as _np
    import concourse.bacc as _bacc
    from concourse import mybir as _mybir
    from concourse.bass_utils import run_bass_kernel_spmd as _run

    nc = _bacc.Bacc("TRN2", target_bir_lowering=False, num_devices=1)
    arrays, args = {}, []
    for name in _INS + ["consts"]:
        a = _consts() if name == "consts" else _np.ascontiguousarray(inputs[name])
        arrays[f"in_{name}"] = a
        args.append(nc.dram_tensor(f"in_{name}", a.shape, _mybir.dt.from_np(a.dtype), kind="ExternalInput").ap())
    args.append(nc.dram_tensor("out_0", (B, 1), _mybir.dt.float32, kind="ExternalOutput").ap())
    build(nc, *args)
    r = _run(nc, [arrays], core_ids=[0])
    return r.results[0]["out_0"]
```

```python
import concourse.bass as bass
from concourse import mybir
from contextlib import ExitStack
import math

P = 128
B = 1024
NS = 26
ND = 13
N = NS + ND
D = 16
V = 100000
F = 128
NT = B // P
NPAIR = NT // 2
DG = 4
NG = D // DG
CW = DG * P
NCH = 2 * NG
ROT = 21
RPT = 3
KT = ROT // RPT
NF = 3
SHIFT = 9
DOWN = 2 * RPT
KR = RPT * N
GR = KR + DOWN
KQ = 2 * N
SLOT = N + 1
XR = 2 * SLOT + 1
EW = SLOT * D
DIN = NS * D + ND
H1, H2, H3 = 1024, 512, 256
K0, K1, K2, K3 = 4, H1 // P, H2 // P, H3 // P
KLAST = DIN - (K0 - 1) * P
PW = 2 * P
ROWS = [K1, K2, K3] * 3 + [K3]
AT = [sum(ROWS[:i]) for i in range(len(ROWS) + 1)]
NPRM = AT[-1]
WO = AT[9]
RSQ = 1.0 / math.sqrt(1.0 + 1e-5)
LA = 4
RING = 7
assert RING > LA and (NCH * KT) % RING == 0
NW = 96
PLAN = {(c, 2): ("xt", c + 2) for c in range(NCH)} | {(c, 5): ("s2", c + 2) for c in range(NCH)}
PLAN |= {(c, 3): ("dn", (c + 2) // NG) for c in (NG - 2, 2 * NG - 2)}
PLAN |= {(3, 0): ("out", 1, 0), (3, 3): ("out", 1, 1), (3, 4): ("out", 1, 2), (3, 6): ("out", 1, 3),
         (4, 0): ("out", 1, 4), (4, 3): ("out", 1, 5), (4, 4): ("out", 1, 6), (4, 6): ("out", 1, 7),
         (5, 6): ("out", 2, 0), (6, 0): ("out", 2, 1), (6, 4): ("out", 2, 2), (6, 6): ("out", 2, 3),
         (7, 4): ("out", 3, 0), (7, 6): ("out", 3, 1)}
SPLITS = {(4, 2): (1, 0, K1 // 2), (5, 2): (1, K1 // 2, K1 // 2), (7, 1): (2, 0, K2)}
SW = N + ROT - 2
TB = 11
SELW = NF * KR + GR
assert KT == 7 and SHIFT == 3 * RPT and ROT == 2 * SHIFT + RPT


def first_rotation(k):
    return k // 3 * SHIFT + (2 - k % 3) * RPT if k < KT - 1 else 2 * SHIFT


def kept(final, job):
    return job[0] == "out" or not final or job[1] < (2 if job[0] == "dn" else NCH)


def build(nc, dense_x, discrete_x, lin_emb, emb_W, dense_W, dense_b, W1, b1, g1, be1, W2, b2, g2, be2,
          W3, b3, g3, be3, Wout, bout, dense_proj, cin_W0, cin_W1, cin_W2, cin_out_W, cin_out_b,
          consts, out):
    fp32 = mybir.dt.float32
    fr = mybir.dt.float32r
    i32 = mybir.dt.int32
    ALU = mybir.AluOpType
    ACT = mybir.ActivationFunctionType
    AX = mybir.AxisListType

    emb_rows = emb_W.rearrange("f v d -> (f v) d")
    lin_rows = lin_emb.rearrange("f v d -> (f v) d")

    with ExitStack() as ctx:
        def sb(name, shape, dt=fp32):
            return ctx.enter_context(nc.sbuf_tensor(name, shape, dt))

        def pb(name, shape, dt=fp32):
            return ctx.enter_context(nc.psum_tensor(name, shape, dt))

        def sem(name):
            return ctx.enter_context(nc.semaphore(name))

        ident = sb("ident", [P, P])
        identr = sb("identr", [P, P], fr)
        cst = sb("cst", [XR, SELW])
        sel = sb("sel", [XR, SELW], fr)
        ones = sb("ones", [P, 1])
        cinw = sb("cinw", [P, 3])
        prm = sb("prm", [P, NPRM])
        scale = sb("scale", [P, K1 + K2 + K3])
        shift = sb("shift", [P, K1 + K2 + K3])
        scalars = sb("scalars", [P, 3])
        bias = sb("bias", [P, 1])
        proj = sb("proj", [P, ND, D])
        dW = sb("dW", [P, ND])
        AH = sb("AH", [KR, KT, P], fr)
        AL = sb("AL", [KR, KT, P], fr)
        BH = sb("BH", [KR, KT, P], fr)
        BL = sb("BL", [KR, KT, P], fr)
        W1H = sb("W1H", [P, K0, H1], fr)
        W2H = sb("W2H", [P, K1, H2], fr)
        W3H = sb("W3H", [P, K2, H3], fr)
        with ExitStack() as early:
            d1raw, d2raw, d3raw = [early.enter_context(nc.sbuf_tensor(name, shape, fp32)) for name, shape in (
                ("d1raw", [P, K0, H1]), ("d2raw", [P, K1, H2]), ("d3raw", [P, K2, H3]))]
        W1L = sb("W1L", [P, K0, H1], fr)
        W2L = sb("W2L", [P, K1, H2], fr)
        W3L = sb("W3L", [P, K2, H3], fr)
        A0H = sb("A0H", [P, K0, PW], fr)
        A0L = sb("A0L", [P, K0, PW], fr)
        idx = sb("idx", [P, NT, NS], i32)
        idx_emb = sb("idx_emb", [P, 2, NS], i32)
        idx_lin = sb("idx_lin", [P, 2, NS], i32)
        dns = sb("dns", [P, NT, ND])
        L = sb("L", [P, 2, NS])
        lin = sb("lin", [P, NPAIR, 2, NS])
        dlin = sb("dlin", [P, NT, ND])
        E = [sb(f"E{p}", [P, EW]) for p in range(2)]
        EE = [sb(f"EE{p}", [P, D, XR], fr) for p in range(2)]
        XT = [sb(f"XT{p}", [XR, CW], fr) for p in range(2)]
        S2 = [sb(f"S2{p}", [GR, CW]) for p in range(2)]
        S1 = sb("S1", [KR, CW])
        S0 = sb("S0", [KR, CW])
        with ExitStack() as early:
            w2col = early.enter_context(nc.sbuf_tensor("w2col", [P, NW], fp32))
            Vx = early.enter_context(nc.sbuf_tensor("Vx", [P, NW], fp32))
        Q = [sb(f"Q{s}", [KR, CW]) for s in range(4)]
        A0 = sb("A0", [P, K0, P])
        lsum = sb("lsum", [P, NT])
        dsum = sb("dsum", [P, NT])
        base = sb("base", [P, NT])
        res = sb("res", [P, NT])
        with ExitStack() as early:
            def eb(name, shape, dt=fp32):
                return early.enter_context(nc.sbuf_tensor(name, shape, dt))
            prm_rows = eb("prm_rows", [NPRM, P])
            byrow = eb("byrow", [P, N * (SW + 1)])
            bycol = eb("bycol", [P, N * (SW + 1)])
            rotw = eb("rotw", [P, ROT, N])
            w0raw = eb("w0raw", [P, N * N])
        QH = [sb(f"QH{s}", [KR, CW], fr) for s in range(RING)]
        QL = [sb(f"QL{s}", [KR, CW], fr) for s in range(RING)]
        with ExitStack() as early:
            raw = eb("raw", [P, 2 * F * N])
        w2raw, w1raw = raw[:, 0:F * N], raw[:, F * N:2 * F * N]
        x1 = sb("x1", [P, CW])
        A1 = sb("A1", [P, K1, PW])
        A1H = sb("A1H", [P, K1, PW], fr)
        A1L = sb("A1L", [P, K1, PW], fr)
        A2, A2H, A2L = A1[:, 0:K2, :], A1H[:, 0:K2, :], A1L[:, 0:K2, :]
        A3 = sb("A3", [P, K3, NPAIR, PW])
        red = sb("red", [P, NT, P])
        redc = sb("redc", [P, P])

        psS = [pb(f"psS{s}", [P, 512]) for s in range(2)]
        psR = [pb(f"psR{s}", [P, 512]) for s in range(2)]
        psA = [pb(f"psA{s}", [P, 512]) for s in range(2)]
        psB = [pb(f"psB{s}", [P, 512]) for s in range(2)]

        idx_in = sem("idx_in")
        w2_in = sem("w2_in")
        w1_in = sem("w1_in")
        w0_in = sem("w0_in")
        cinw_in = sem("cinw_in")
        prm_in = sem("prm_in")
        id_in = sem("id_in")
        cst_in = sem("cst_in")
        dense_in = sem("dense_in")
        small_in = sem("small_in")
        d1_in = sem("d1_in")
        d2_in = sem("d2_in")
        d2_rest_in = sem("d2_rest_in")
        d3_in = sem("d3_in")
        emb_in = [sem(f"emb_in{p}") for p in range(2)]
        lin_in = sem("lin_in")
        s1_in = sem("s1_in")
        s0_in = sem("s0_in")
        out_st = sem("out_st")
        pool_step = sem("pool_step")
        pool_go = sem("pool_go")
        lin_done = sem("lin_done")
        ones_set = sem("ones_set")
        prm_ps = sem("prm_ps")
        prm_sb = sem("prm_sb")
        aff = sem("aff")
        aff_done = sem("aff_done")
        w2_col = sem("w2_col")
        v_ps = sem("v_ps")
        v_sb = sem("v_sb")
        t_ps = sem("t_ps")
        sq_done = sem("sq_done")
        rotw_done = sem("rotw_done")
        rt_ps = sem("rt_ps")
        rt_hi = sem("rt_hi")
        rt_lo = sem("rt_lo")
        sel_done = sem("sel_done")
        wh_done = sem("wh_done")
        wh1_done = sem("wh1_done")
        wh2_done = sem("wh2_done")
        wh3_done = sem("wh3_done")
        wl_done = sem("wl_done")
        prod_done = sem("prod_done")
        hi_done = sem("hi_done")
        lo_done = sem("lo_done")
        st_full = sem("st_full")
        st_free = sem("st_free")
        rot_full = sem("rot_full")
        mul_done = sem("mul_done")
        qh_done = sem("qh_done")
        ql_done = sem("ql_done")
        acc_done = sem("acc_done")
        x1_done = sem("x1_done")
        xy_done = sem("xy_done")
        red_done = sem("red_done")
        tot_done = sem("tot_done")
        in_h = sem("in_h")
        in_l = sem("in_l")
        act_h = sem("act_h")
        act_l = sem("act_l")
        fin_ps = sem("fin_ps")
        fin_sb = sem("fin_sb")

        block = ctx.enter_context(nc.Block())

        jobs = [("xt", 0), ("s2", 0), ("dn", 0), ("xt", 1), ("s2", 1)]
        before = len(jobs)
        jobs += [PLAN[c, k] for c in range(NCH) for k in range(KT) if (c, k) in PLAN]
        job = {name: n for n, name in enumerate(jobs)}
        STP = len(jobs) - before
        last_jobs = [x for x in jobs if kept(True, x)]
        last_job = {name: n for n, name in enumerate(last_jobs)}
        assert STP % 2 == 0
        assert all(job[kind, n + m] - STP <= job[kind, n]
                   for kind, n, m in (("xt", 0, NCH), ("xt", 1, NCH), ("s2", 0, NCH), ("s2", 1, NCH),
                                    ("dn", 0, 2)))

        def number(i, name):
            return (last_job if isinstance(i, int) and i == NPAIR - 1 else job)[name]

        def emptied(i, *name):
            return STP * i + number(i, name) + 1

        def rt_bank(r):
            which, k = divmod(r, KT)
            ring = ([psR[0], psR[1], psS[0], psS[1]], [psA[0], psB[0], psA[1], psB[1]])[which]
            return ring[k % len(ring)], r - len(ring) if k >= len(ring) else None

        def high_weights(copy, layer, k, m):
            raw, high = ((d1raw, W1H), (d2raw, W2H), (d3raw, W3H))[layer - 1]
            rows = KLAST if layer == 1 and k + m == K0 else P
            return copy(high[0:rows, k:k + m, :], raw[0:rows, k:k + m, :])

        @block.sync
        def _(sp):
            sp.dma_start(idx[:, :, :], discrete_x.rearrange("(p t) f -> p t f", t=NT)).then_inc(idx_in, 16)
            sp.dma_start(w2raw, cin_W2.rearrange("g f m -> g (f m)")).then_inc(w2_in, 16)
            sp.dma_start(w0raw[:, :], cin_W0.rearrange("f m n -> f (m n)")).then_inc(w0_in, 16)
            sp.dma_start(ident[:, :], consts[:, SELW:SELW + P]).then_inc(id_in, 16)
            sp.dma_start(w1raw, cin_W1.rearrange("f c n -> f (c n)")).then_inc(w1_in, 16)
            sp.dma_start(cst[:, :], consts[0:XR, 0:SELW]).then_inc(cst_in, 16)
            sp.dma_start(dns[:, :, :], dense_x.rearrange("(p t) f -> p t f", t=NT)).then_inc(dense_in, 16)
            sp.dma_start(proj[:, :, :].rearrange("p j d -> p (j d)"),
                         dense_proj.rearrange("j d -> (j d)").partition_broadcast(P)).then_inc(dense_in, 16)
            sp.wait_ge(w2_in, 16)
            sp.dma_start(d1raw[:, 0:K0 - 1, :],
                         W1[0:(K0 - 1) * P, :].rearrange("(k p) n -> p k n", p=P)).then_inc(d1_in, 16)
            sp.dma_start(d1raw[0:KLAST, K0 - 1, :], W1[(K0 - 1) * P:DIN, :]).then_inc(d1_in, 16)
            sp.dma_start(d3raw[:, :, :], W3.rearrange("(k p) n -> p k n", p=P)).then_inc(d3_in, 16)
            w2k = W2.rearrange("(k p) n -> p k n", p=P)
            sp.dma_start(d2raw[:, 0:K1 // 2, :], w2k[:, 0:K1 // 2, :]).then_inc(d2_in, 16)
            sp.wait_ge(emb_in[0], 16 * NS)
            sp.dma_start(d2raw[:, K1 // 2:K1, :], w2k[:, K1 // 2:K1, :]).then_inc(d2_rest_in, 16)
            sp.dma_start(dW[:, :], dense_W.rearrange("j o -> (j o)").partition_broadcast(P)).then_inc(small_in, 16)
            for j, src in enumerate((dense_b, bout, cin_out_b)):
                sp.dma_start(scalars[:, j:j + 1], src.partition_broadcast(P)).then_inc(small_in, 16)

            def shifted(i, c):
                done = KT * (NCH * i + c - 1)
                sp.wait_ge(st_free, emptied(i, "s2", c))
                for v, dst, filled in ((1, S1, s1_in), (0, S0, s0_in)):
                    if not (isinstance(i, int) and i == c == 0):
                        sp.wait_ge(mul_done, done + 6 - v)
                    rows = (2 - v) * RPT
                    sp.dma_start(dst[:, :], S2[c % 2][rows:rows + KR, :]).then_inc(filled, 16)

            shifted(0, 0)
            with sp.Fori(0, NPAIR - 1) as i:
                for c in range(NCH):
                    shifted(i, c + 1)
            for c in range(NCH - 1):
                shifted(NPAIR - 1, c + 1)
            sp.wait_ge(fin_sb, 1)
            sp.dma_start(out.rearrange("(p t) o -> p (t o)", t=NT), res[:, :]).then_inc(out_st, 16)
            sp.wait_ge(out_st, 16)

        @block.gpsimd
        def _(pool):
            def gather(dst, idx_col, rows, f, done):
                pool.indirect_dma_start(dst, None, rows, bass.IndirectOffsetOnAxis(ap=idx_col, axis=0),
                                        element_offset=f * V * rows.shape[1]).then_inc(done, 16)

            def gather_lin(dst):
                for p in range(2):
                    for f in range(NS):
                        gather(dst[:, p, f:f + 1], idx_lin[:, p, f:f + 1], lin_rows, f, lin_in)

            def gather_emb_next(i, copied):
                for p in range(2):
                    pool.wait_ge(emb_in[p], 16 * NS * i + 16 * NS)
                nc.gpsimd.tensor_copy(idx_emb[:, :, :], idx[:, bass.ds(2 * i + 2, 2), :]).then_inc(pool_step, 1)
                pool.wait_ge(pool_step, copied)
                for p in range(2):
                    pool.wait_ge(lo_done, 2 * i + p + 1)
                    pool.wait_ge(st_free, emptied(i, "dn", p))
                    pool.sem_inc(pool_go, 1)
                    for f in range(NS):
                        gather(E[p][:, f * D:(f + 1) * D], idx_emb[:, p, f:f + 1], emb_rows, f, emb_in[p])

            pool.wait_ge(idx_in, 16)
            nc.gpsimd.tensor_copy(idx_emb[:, :, :], idx[:, 0:2, :]).then_inc(pool_step, 1)
            nc.gpsimd.tensor_copy(idx_lin[:, :, :], idx[:, 0:2, :]).then_inc(pool_step, 1)
            pool.wait_ge(pool_step, 2)
            for p in range(2):
                for f in range(NS):
                    gather(E[p][:, f * D:(f + 1) * D], idx_emb[:, p, f:f + 1], emb_rows, f, emb_in[p])
            sub = nc.gpsimd.tensor_tensor
            pool.wait_ge(wh_done, 1)
            pool.wait_ge(wh1_done, 1)
            sub(W1L[:, 0:K0 - 1, :], d1raw[:, 0:K0 - 1, :], W1H[:, 0:K0 - 1, :].bitcast(fp32),
                ALU.subtract)
            sub(W1L[0:KLAST, K0 - 1, :], d1raw[0:KLAST, K0 - 1, :],
                W1H[0:KLAST, K0 - 1, :].bitcast(fp32), ALU.subtract).then_inc(wl_done, 1)
            pool.wait_ge(wh_done, 2)
            pool.wait_ge(wh2_done, 1)
            sub(W2L[:, :, :], d2raw[:, :, :], W2H[:, :, :].bitcast(fp32), ALU.subtract).then_inc(wl_done, 1)
            pool.wait_ge(wh3_done, 1)
            sub(W3L[:, :, :], d3raw[:, :, :], W3H[:, :, :].bitcast(fp32), ALU.subtract).then_inc(wl_done, 1)
            gather_emb_next(0, 3)
            gather_lin(L)
            with pool.Fori(1, NPAIR - 1) as i:
                gather_emb_next(i, 3 * i + 1)
                pool.wait_ge(lin_in, 2 * 16 * NS * i)
                nc.gpsimd.tensor_copy(lin[:, bass.ds(i - 1, 1), :, :].rearrange("p a t f -> p (a t) f"),
                                      L[:, :, :]).then_inc(pool_step, 1)
                nc.gpsimd.tensor_copy(idx_lin[:, :, :], idx[:, bass.ds(2 * i, 2), :]).then_inc(pool_step, 1)
                pool.wait_ge(pool_step, 3 * i + 3)
                pool.sem_inc(pool_go, 1)
                gather_lin(L)
            pool.wait_ge(lin_in, 2 * 16 * NS * (NPAIR - 1))
            nc.gpsimd.tensor_copy(lin[:, NPAIR - 2, :, :], L[:, :, :]).then_inc(lin_done, 1)
            nc.gpsimd.tensor_copy(idx_lin[:, :, :], idx[:, 2 * NPAIR - 2:2 * NPAIR, :]).then_inc(pool_step, 1)
            pool.wait_ge(pool_step, 3 * (NPAIR - 1) + 1)
            gather_lin(lin[:, NPAIR - 1, :, :])

        @block.tensor
        def _(pe):
            mm = nc.tensor.matmul

            def rotations(which, tiles):
                pe.wait_ge(rotw_done, which + 1)
                for k in tiles:
                    r = which * KT + k
                    lo = first_rotation(k)
                    bank, before = rt_bank(r)
                    if before is not None:
                        pe.wait_ge(rt_lo, before + 1)
                    nc.tensor.transpose(bank[0:KR, 0:P],
                                        rotw[:, lo:lo + RPT, :].rearrange("c r i -> c (r i)"),
                                        ident[:, :]).then_inc(rt_ps, 1)

            pe.wait_ge(w2_col, 1)
            pe.wait_ge(w2_in, 16)
            w2v = w2raw.rearrange("g (f m) -> g m f", m=N)
            for m in range(N):
                last = mm(psS[1][:, m:m + NW], w2v[:, m, :], w2col[:, :], start=True, stop=True)
            last.then_inc(v_ps, 1)
            pe.wait_ge(v_sb, 1)
            pe.wait_ge(w1_in, 16)
            w1v = w1raw.rearrange("f (c n) -> f n c", n=N)
            tb = [psA[0], psB[0], psA[1], psB[1]]
            for n in range(N):
                j = n % TB * SLOT
                last = mm(tb[n // TB][:, j:j + NW], w1v[:, n, :], Vx[:, :], start=True, stop=True)
                if (n + 1) % TB == 0 or n + 1 == N:
                    last.then_inc(t_ps, 1)
                if n + 1 == TB:
                    pe.wait_ge(id_in, 16)
                    rotations(0, range(4))
                elif n + 1 == 2 * TB:
                    rotations(0, range(4, KT))
                elif n + 1 == 3 * TB:
                    pe.wait_ge(prm_in, 16 * len(ROWS))
                    pe.wait_ge(rt_lo, KT)
                    nc.tensor.transpose(psS[0][:, 0:NPRM], prm_rows[:, :], ident[0:NPRM, 0:NPRM]).then_inc(prm_ps, 1)

            def stage_bank(i, *name):
                n = number(i, name)
                if n >= 2:
                    pe.wait_ge(st_free, STP * i + n - 1)
                return psS[n % 2]

            def x_transpose(i, c):
                p, g = c // NG % 2, c % NG
                if g == 0:
                    pe.wait_ge(lo_done, 2 * i + c // NG + 1)
                ps = stage_bank(i, "xt", c)
                for d in range(DG):
                    last = mm(ps[0:XR, d * P:(d + 1) * P], EE[p][:, g * DG + d, :], identr[:, :],
                              start=True, stop=True)
                last.then_inc(st_full, 1)

            def dnn_transpose(i, t):
                ps = stage_bank(i, "dn", t)
                for k in range(K0):
                    last = nc.tensor.transpose(ps[:, k * P:(k + 1) * P], E[t % 2][:, k * P:(k + 1) * P], ident[:, :])
                last.then_inc(st_full, 1)

            def s2_factor(i, c):
                pe.wait_ge(st_free, emptied(i, "xt", c))
                ps = stage_bank(i, "s2", c)
                mm(ps[0:GR, :], sel[:, NF * KR:SELW], XT[c % 2][:, :], start=True, stop=True).then_inc(st_full, 1)

            def factor(i, c, u):
                r = NF * c + u
                if u == 0:
                    pe.wait_ge(st_free, emptied(i, "xt", c))
                if r >= 2:
                    tile = KT * ((r - 2) // NF) + min(3 * ((r - 2) % NF) + 2, KT - 1)
                    pe.wait_ge(mul_done, KT * NCH * i + tile + 1)
                mm(psR[r % 2][0:KR, :], sel[:, u * KR:(u + 1) * KR], XT[c % 2][:, :],
                   start=True, stop=True).then_inc(rot_full, 1)

            def products(i, c, k):
                pe.wait_ge(ql_done, KT * (NCH * i + c) + k + 1)
                ka = KQ if k == KT - 1 else KR
                q = (KT * c + k) % RING
                h, l = QH[q][:, :], QL[q][:, :]
                first, lastk = k == 0, k == KT - 1
                mm(psA[c % 2][:, :], AH[0:ka, k, :], h[0:ka, :], start=first, stop=False)
                mm(psA[c % 2][:, :], AH[0:ka, k, :], l[0:ka, :], start=False, stop=False)
                mm(psA[c % 2][:, :], AL[0:ka, k, :], h[0:ka, :], start=False, stop=lastk)
                mm(psB[c % 2][:, :], BH[:, k, :], h, start=first, stop=False)
                mm(psB[c % 2][:, :], BH[:, k, :], l, start=False, stop=False)
                last = mm(psB[c % 2][:, :], BL[:, k, :], h, start=False, stop=lastk)
                if lastk:
                    last.then_inc(acc_done, 1)

            def outputs(i, n, m):
                kk = (K0, K1, K2)[n - 1]
                wh, wl, xh, xl = {1: (W1H, W1L, A0H, A0L), 2: (W2H, W2L, A1H, A1L), 3: (W3H, W3L, A2H, A2L)}[n]
                if m == 0:
                    pe.wait_ge(wl_done, n)
                    if n == 1:
                        pe.wait_ge(in_l, 2 * i + 2)
                    else:
                        pe.wait_ge(act_l, 3 * i + n)
                ps = stage_bank(i, "out", n, m)
                for k in range(kk):
                    rows = KLAST if n == 1 and k == K0 - 1 else P
                    w, v = wh[0:rows, k, m * P:(m + 1) * P], wl[0:rows, k, m * P:(m + 1) * P]
                    mm(ps[:, 0:PW], w, xh[0:rows, k, :], start=k == 0, stop=False)
                    mm(ps[:, 0:PW], w, xl[0:rows, k, :], start=False, stop=False)
                    last = mm(ps[:, 0:PW], v, xh[0:rows, k, :], start=False, stop=k == kk - 1)
                last.then_inc(st_full, 1)

            pe.wait_ge(sel_done, 2)
            pe.wait_ge(prm_sb, 1)
            x_transpose(0, 0)
            s2_factor(0, 0)
            dnn_transpose(0, 0)
            rotations(1, range(4))
            factor(0, 0, 0)
            x_transpose(0, 1)
            rotations(1, range(4, KT))
            factor(0, 0, 1)
            s2_factor(0, 1)
            pe.wait_ge(rt_lo, 2 * KT)

            run = {"xt": x_transpose, "dn": dnn_transpose, "s2": s2_factor, "out": outputs}

            def pair(i, final):
                for c in range(NCH):
                    for k in range(KT):
                        ahead = KT * c + k + LA
                        if ahead % KT % 3 == 0 and not (final and ahead >= KT * NCH):
                            factor(i, ahead // KT, ahead % KT // 3)
                        products(i, c, k)
                        if (c, k) in PLAN and kept(final, PLAN[c, k]):
                            run[PLAN[c, k][0]](i, *PLAN[c, k][1:])
                        if final and c + 1 == NCH and KT - LA <= k < KT - 1:
                            if k == KT - LA:
                                pe.wait_ge(mul_done, KT * NT * NG)
                            for t in (2 * (k - KT + LA), 2 * (k - KT + LA) + 1):
                                logits(psR[0], t).then_inc(fin_ps, 1)

            def logits(bank, t):
                for k in range(K3):
                    mm(bank[:, t:t + 1], A3[:, k, t // 2, t % 2 * P:(t % 2 + 1) * P],
                       prm[:, WO + k:WO + k + 1], start=k == 0, stop=False)
                pe.wait_ge(tot_done, (t + 1) * (NG - 1))
                return mm(bank[:, t:t + 1], red[:, t, :], ones[:, :], start=False, stop=True)

            with pe.Fori(0, NPAIR - 1) as i:
                pair(i, False)
            pair(NPAIR - 1, True)
            pe.wait_ge(st_free, emptied(NPAIR - 1, "out", 3, K3 - 1))
            for t in (NT - 2, NT - 1):
                logits(psR[1], t).then_inc(fin_ps, 1)

        @block.scalar
        def _(act):
            for m in (2, 1, 0):
                act.dma_start(cinw[:, m:m + 1], cin_out_W[m * P:(m + 1) * P, :]).then_inc(cinw_in, 16)
            rows = [b1, b2, b3, g1, g2, g3, be1, be2, be3]
            for j, src in enumerate(rows):
                act.dma_start(prm_rows[AT[j]:AT[j + 1], :], src.rearrange("(m p) -> m p", p=P)).then_inc(prm_in, 16)
            act.dma_start(prm_rows[WO:WO + K3, :], Wout.rearrange("(m p) o -> m (p o)", p=P)).then_inc(prm_in, 16)
            copy = nc.scalar.copy
            rows_of = byrow[:, 0:N * SW].rearrange("c (m n) -> c m n", n=SW)
            cols_of = bycol[:, 0:N * SW].rearrange("c (m n) -> c m n", n=SW)

            def square(src, n0):
                n = src.shape[1]
                turned = src.rearrange("c n m -> c m n")
                copy(rows_of[:, n0:n0 + n, 0:N], src)
                copy(rows_of[:, n0:n0 + n, N:SW], src[:, :, 0:SW - N])
                last = copy(cols_of[:, :, n0:n0 + n], turned)
                w = min(n, SW - N - n0)
                if w > 0:
                    last = copy(cols_of[:, :, N + n0:N + n0 + w], turned[:, :, 0:w])
                return last

            def high_rotations(which, tiles):
                for r in (which * KT + k for k in tiles):
                    act.wait_ge(rt_ps, r + 1)
                    copy((AH, BH)[which][:, r % KT, :], rt_bank(r)[0][0:KR, 0:P]).then_inc(rt_hi, 1)

            def split_high(i, t):
                p = t % 2
                act.wait_ge(emb_in[p], 16 * NS * (i + t // 2 + 1))
                act.wait_ge(prod_done, 2 * i + t + 1)
                nc.scalar.copy(EE[p][:, :, 0:SLOT],
                               E[p][:, :].rearrange("b (n d) -> b d n", d=D)).then_inc(hi_done, 1)

            act.wait_ge(w0_in, 16)
            square(w0raw[:, :].rearrange("c (n m) -> c n m", m=N), 0).then_inc(sq_done, 1)
            act.wait_ge(id_in, 16)
            copy(identr[:, :], ident[:, :]).then_inc(sel_done, 1)
            act.wait_ge(v_ps, 1)
            act.wait_ge(w2_col, 1)
            copy(Vx[:, 0:N], psS[1][:, 0:N]).then_inc(v_sb, 1)
            act.wait_ge(cst_in, 16)
            copy(sel[:, :], cst[:, :]).then_inc(sel_done, 1)
            act.wait_ge(d1_in, 32)
            high_weights(copy, 1, 0, 1)
            act.wait_ge(rotw_done, 1)
            for j, ps in enumerate([psA[0], psB[0], psA[1], psB[1]]):
                n = min(TB, N - j * TB)
                act.wait_ge(t_ps, j + 1)
                bank = ps[:, 0:n * SLOT].rearrange("c (n m) -> c n m", m=SLOT)
                last = square(bank[:, :, 0:N], j * TB)
                if j == 0:
                    high_rotations(0, range(4))
                    high_weights(copy, 1, 1, 1).then_inc(wh_done, 1)
                elif j == 1:
                    high_rotations(0, range(4, KT))
                    act.wait_ge(ones_set, 2)
                    split_high(0, 0)
                elif j == 2:
                    act.wait_ge(prm_ps, 1)
                    copy(prm[:, :], psS[0][:, 0:NPRM]).then_inc(prm_sb, 1)
            for j, ps in enumerate([psA[0], psB[0], psA[1], psB[1]]):
                n = min(TB, N - j * TB)
                col = (j * TB + DOWN) % N
                last = copy(rotw[:, ROT - 1, col:col + n],
                            ps[:, 0:n * SLOT].rearrange("c (n m) -> c n m", m=SLOT)[:, :, N])
            last.then_inc(sq_done, 1)

            def full(i, *name):
                n = number(i, name)
                act.wait_ge(st_full, STP * i + n + 1)
                return psS[n % 2]

            def round_high(i, c, k):
                r = KT * c + k
                act.wait_ge(mul_done, KT * NCH * i + r + 1)
                copy(QH[r % RING][:, :], Q[r % 4][:, :]).then_inc(qh_done, 1)

            def empty_xt(i, c):
                copy(XT[c % 2][:, :], full(i, "xt", c)[0:XR, :]).then_inc(st_free, 1)

            def empty_s2(i, c):
                copy(S2[c % 2][:, :], full(i, "s2", c)[0:GR, :]).then_inc(st_free, 1)

            def empty_dnn(i, t):
                ps = full(i, "dn", t)
                if t:
                    act.wait_ge(in_l, 2 * i + t)
                copy(A0[:, :, :].rearrange("a k b -> a (k b)"), ps[:, :]).then_inc(st_free, 1)

            def high_dnn_input(i, t):
                p = t % 2
                act.wait_ge(st_free, emptied(i, "dn", t))
                copy(A0H[:, :, p * P:(p + 1) * P], A0[:, :, :]).then_inc(in_h, 1)

            def relu(i, n, m):
                o = (0, K1, K1 + K2)[n - 1] + m
                if n == 3:
                    dst = A3[:, m, bass.ds(i, 1), :].rearrange("c a b -> c (a b)")
                else:
                    dst = (A1, A2)[n - 1][:, m, :]
                nc.scalar.activation(dst, full(i, "out", n, m)[:, 0:PW], ACT.Relu, bias=shift[:, o:o + 1],
                                     scale=scale[:, o:o + 1]).then_inc(st_free, 1)

            def high_activations(i, n, m0, mt):
                act.wait_ge(st_free, emptied(i, "out", n, m0 + mt - 1))
                src, dst = ((A1, A1H), (A2, A2H))[n - 1]
                copy(dst[:, m0:m0 + mt, :], src[:, m0:m0 + mt, :]).then_inc(act_h, 1)

            run = {"xt": empty_xt, "dn": empty_dnn, "s2": empty_s2, "out": relu}

            empty_xt(0, 0)
            empty_s2(0, 0)
            empty_dnn(0, 0)
            high_rotations(1, range(4))
            empty_xt(0, 1)
            high_rotations(1, range(4, KT))
            round_high(0, 0, 0)
            round_high(0, 0, 1)
            empty_s2(0, 1)
            high_dnn_input(0, 0)
            for k in range(2, LA):
                round_high(0, 0, k)
            act.wait_ge(d2_rest_in, 16)
            high_weights(copy, 2, K1 // 2, K1 // 2).then_inc(wh_done, 1)
            act.wait_ge(aff_done, 1)

            def pair(i, final):
                def empty(c, k):
                    if (c, k) in PLAN and kept(final, PLAN[c, k]):
                        run[PLAN[c, k][0]](i, *PLAN[c, k][1:])

                for c in range(NCH):
                    for k in range(KT):
                        ahead = KT * c + k + LA
                        if not (final and ahead >= KT * NCH):
                            round_high(i, *divmod(ahead, KT))
                        if k == 1 and c + 3 in (NG, 2 * NG) and not (final and c + 3 == 2 * NG):
                            split_high(i, (c + 3) // NG)
                        if k:
                            empty(c, k - 1)
                        if (c, k) in SPLITS:
                            high_activations(i, *SPLITS[c, k])
                        if k == 5 and PLAN.get((c, 3), ("",))[0] == "dn" and not (final and c + 2 >= NCH):
                            high_dnn_input(i, (c + 2) // NG)
                    act.wait_ge(acc_done, NCH * i + c + 1)
                    copy(x1[:, :], psA[c % 2][:, :]).then_inc(x1_done, 1)
                    empty(c, KT - 1)

            with act.Fori(0, NPAIR - 1) as i:
                pair(i, False)
            pair(NPAIR - 1, True)

        @block.vector
        def _(dve):
            tt = nc.vector.tensor_tensor
            nc.vector.memset(w2col[:, :], 0.0)
            nc.vector.memset(Vx[:, :], 0.0)
            nc.vector.memset(ones[:, :], 1.0).then_inc(ones_set, 1)
            dve.wait_ge(ones_set, 1)
            for p in range(2):
                nc.vector.memset(E[p][:, DIN:SLOT * D - ND * D], 0.0)
                last = nc.vector.tensor_copy(EE[p][:, :, XR - 1:XR],
                                             ones[:, :].rearrange("p (a b) -> p a b", a=1).broadcast_to([P, D, 1]))
            last.then_inc(ones_set, 1)

            rows_of = byrow[:, :].rearrange("c (i j) -> c j i", i=N)
            cols_of = bycol[:, :].rearrange("c (i j) -> c j i", i=N)

            def rotations(which):
                dve.wait_ge(sq_done, which + 1)
                nc.vector.tensor_copy(rotw[:, 0, :], rows_of[:, 0, :])
                rot = rotw[:, 0:2 * SHIFT, :].rearrange("c (u r) i -> c u r i", u=2)
                row = rows_of[:, 0:2 * SHIFT, :].rearrange("c (u r) i -> c u r i", u=2)
                col = cols_of[:, 0:2 * SHIFT, :].rearrange("c (u r) i -> c u r i", u=2)
                tt(rotw[:, 1:RPT, :], rows_of[:, 1:RPT, :], cols_of[:, 1:RPT, :], ALU.add)
                tt(rot[:, 1, 0:RPT, :], row[:, 1, 0:RPT, :], col[:, 1, 0:RPT, :], ALU.add)
                for shift, dst, one, other in (
                        (RPT, rot[:, :, RPT:2 * RPT, :], row[:, :, RPT:2 * RPT, :], col[:, :, RPT:2 * RPT, :]),
                        (DOWN, rot[:, :, DOWN:SHIFT, :], row[:, :, DOWN:SHIFT, :], col[:, :, DOWN:SHIFT, :]),
                        (DOWN, *(x[:, 2 * SHIFT:ROT - 1, :].rearrange("c (u r) i -> c u r i", u=1)
                                 for x in (rotw, rows_of, cols_of)))):
                    for a, b, n in ((0, shift, N - shift), (N - shift, 0, shift)):
                        last = tt(dst[:, :, :, b:b + n], one[:, :, :, a:a + n], other[:, :, :, a:a + n], ALU.add)
                last.then_inc(rotw_done, 1)

            def low_rotations(which, tiles):
                lo, hi = ((AL, AH), (BL, BH))[which]
                for r in (which * KT + k for k in tiles):
                    dve.wait_ge(rt_hi, r + 1)
                    tt(lo[:, r % KT, :], rt_bank(r)[0][0:KR, 0:P], hi[:, r % KT, :].bitcast(fp32),
                       ALU.subtract).then_inc(rt_lo, 1)

            def dense_parts(i, t):
                p = t % 2
                x = dns[:, bass.ds(2 * i + t, 1), :].rearrange("b a j -> b (a j)")
                nc.vector.tensor_copy(E[p][:, NS * D:DIN], x)
                tt(E[p][:, (NS + 1) * D:].rearrange("b (j d) -> b j d", d=D),
                   dns[:, bass.ds(2 * i + t, 1), :].rearrange("b a j -> b j a").broadcast_to([P, ND, D]),
                   proj[:, :, :], ALU.mult).then_inc(prod_done, 1)

            nc.vector.memset(rotw[:, ROT - 1, :], 0.0)
            dve.wait_ge(cinw_in, 48)
            nc.vector.tensor_copy(Vx[:, N:SLOT], cinw[:, 1:2])
            nc.vector.tensor_copy(w2col[:, 0:1], cinw[:, 2:3]).then_inc(w2_col, 1)
            rotations(0)
            dve.wait_ge(dense_in, 32)
            dense_parts(0, 0)
            dve.wait_ge(d1_in, 32)
            high_weights(nc.vector.tensor_copy, 1, 2, 1)
            high_weights(nc.vector.tensor_copy, 1, 3, 1).then_inc(wh1_done, 1)
            low_rotations(0, range(KT))
            dve.wait_ge(d3_in, 16)
            high_weights(nc.vector.tensor_copy, 3, 0, K2).then_inc(wh3_done, 1)

            def split_low(i, t):
                p = t % 2
                dve.wait_ge(hi_done, 2 * i + t + 1)
                tt(EE[p][:, :, SLOT:2 * SLOT], E[p][:, :].rearrange("b (n d) -> b d n", d=D),
                   EE[p][:, :, 0:SLOT].bitcast(fp32), ALU.subtract).then_inc(lo_done, 1)

            def multiply(i, c, k):
                r = KT * c + k
                u, v = k // 3, 2 - k % 3
                chunk = NCH * i + c
                if k == 0:
                    dve.wait_ge(st_free, emptied(i, "s2", c))
                elif k < 3:
                    dve.wait_ge((s0_in, s1_in)[v], 16 * chunk + 16)
                if k % 3 == 0:
                    dve.wait_ge(rot_full, NF * chunk + u + 1)
                if r >= 4:
                    dve.wait_ge(ql_done, KT * NCH * i + r - 3)
                tt(Q[r % 4][:, :], psR[(NF * c + u) % 2][0:KR, :], (S0, S1, S2[c % 2])[v][0:KR, :],
                   ALU.mult).then_inc(mul_done, 1)

            def subtract(i, c, k):
                r = KT * c + k
                dve.wait_ge(qh_done, KT * NCH * i + r + 1)
                tt(QL[r % RING][:, :], Q[r % 4][:, :], QH[r % RING][:, :].bitcast(fp32),
                   ALU.subtract).then_inc(ql_done, 1)

            def chunk_sum(i, c):
                dve.wait_ge(x1_done, NCH * i + c + 1)
                nc.vector.scalar_tensor_tensor(x1[:, :], psB[c % 2][:, :], cinw[:, 0:1], x1[:, :],
                                               ALU.add, ALU.mult).then_inc(xy_done, 1)
                dve.wait_ge(xy_done, NCH * i + c + 1)
                total = red[:, bass.ds(2 * i + c // NG, 1), :].rearrange("c a b -> c (a b)")
                part = total if c % NG == 0 else redc[:, :]
                nc.vector.tensor_reduce(part, x1[:, :].rearrange("c (d b) -> c b d", d=DG), AX.X,
                                        ALU.add).then_inc(red_done, 1)
                if c % NG:
                    dve.wait_ge(red_done, NCH * i + c + 1)
                    tt(total, total, redc[:, :], ALU.add).then_inc(tot_done, 1)

            def low_dnn_input(i, t):
                dve.wait_ge(in_h, 2 * i + t + 1)
                s = slice(t % 2 * P, (t % 2 + 1) * P)
                tt(A0L[:, :, s], A0[:, :, :], A0H[:, :, s].bitcast(fp32), ALU.subtract).then_inc(in_l, 1)

            def low_activations(i, piece, n, m0, mt):
                dve.wait_ge(act_h, 3 * i + piece + 1)
                x, h, l = ((A1, A1H, A1L), (A2, A2H, A2L))[n - 1]
                tt(l[:, m0:m0 + mt, :], x[:, m0:m0 + mt, :], h[:, m0:m0 + mt, :].bitcast(fp32),
                   ALU.subtract).then_inc(act_l, 1)

            split_low(0, 0)
            dve.wait_ge(d2_in, 16)
            high_weights(nc.vector.tensor_copy, 2, 0, K1 // 2).then_inc(wh2_done, 1)
            rotations(1)
            low_rotations(1, range(4))
            multiply(0, 0, 0)
            low_rotations(1, range(4, KT))
            dve.wait_ge(prm_sb, 1)
            nc.vector.tensor_scalar(scale[:, :], prm[:, AT[3]:AT[6]], RSQ, None, ALU.mult).then_inc(aff, 1)
            dve.wait_ge(aff, 1)
            tt(shift[:, :], prm[:, AT[0]:AT[3]], scale[:, :], ALU.mult).then_inc(aff, 1)
            dve.wait_ge(aff, 2)
            tt(shift[:, :], shift[:, :], prm[:, AT[6]:AT[9]], ALU.add).then_inc(aff_done, 1)
            subtract(0, 0, 0)
            multiply(0, 0, 1)
            for k in range(2, LA):
                multiply(0, 0, k)
                subtract(0, 0, k - 1)
            low_dnn_input(0, 0)

            def pair(i, final):
                for c in range(NCH):
                    t = (c + 3) // NG

                    def between(k):
                        if k == 0 and c % NG == 0 and not (final and c == NG):
                            dense_parts(i, c // NG + 1)
                        if k == 2 and c + 3 in (NG, 2 * NG) and not (final and t == 2):
                            split_low(i, t)
                        if (c, k - 1) in SPLITS:
                            low_activations(i, list(SPLITS).index((c, k - 1)), *SPLITS[c, k - 1])
                        if k == 6 and PLAN.get((c, 3), ("",))[0] == "dn" and not (final and c + 2 >= NCH):
                            low_dnn_input(i, (c + 2) // NG)

                    for k in range(KT):
                        ahead = KT * c + k + LA
                        if k and not (final and ahead >= KT * NCH):
                            multiply(i, *divmod(ahead, KT))
                        if not (final and ahead > KT * NCH):
                            subtract(i, *divmod(ahead - 1, KT))
                        between(k)
                    if not (final and c + 1 == NCH):
                        multiply(i, c + 1, LA)
                    chunk_sum(i, c)

            multiply(0, 0, LA)
            with dve.Fori(0, NPAIR - 1) as i:
                pair(i, False)
            pair(NPAIR - 1, True)

            dve.wait_ge(small_in, 4 * 16)
            dve.wait_ge(lin_done, 1)
            dve.wait_ge(lin_in, 2 * 16 * NS * NPAIR)
            nc.vector.tensor_reduce(lsum[:, :], lin[:, :, :, :].rearrange("b q t f -> b (q t) f"), AX.X,
                                    ALU.add).then_inc(aff, 1)
            tt(dlin[:, :, :], dns[:, :, :], dW[:, :].rearrange("b (a j) -> b a j", a=1).broadcast_to([P, NT, ND]),
               ALU.mult).then_inc(aff, 1)
            nc.vector.tensor_reduce(bias[:, :], scalars[:, :], AX.X, ALU.add).then_inc(aff, 1)
            dve.wait_ge(aff, 5)
            nc.vector.tensor_reduce(dsum[:, :], dlin[:, :, :], AX.X, ALU.add).then_inc(aff, 1)
            dve.wait_ge(aff, 6)
            nc.vector.scalar_tensor_tensor(base[:, :], lsum[:, :], bias[:, 0:1], dsum[:, :], ALU.add,
                                           ALU.add).then_inc(aff, 1)
            dve.wait_ge(aff, 7)
            dve.wait_ge(fin_ps, NT - 2)
            tt(res[:, 0:NT - 2], psR[0][:, 0:NT - 2], base[:, 0:NT - 2], ALU.add)
            dve.wait_ge(fin_ps, NT)
            tt(res[:, NT - 2:NT], psR[1][:, NT - 2:NT], base[:, NT - 2:NT], ALU.add).then_inc(fin_sb, 1)


def _consts():
    import numpy as np
    c = np.zeros((P, SELW + P), np.float32)
    slot = [f if f < NS else f + 1 for f in range(N)]
    for u in range(NF):
        for j in range(RPT):
            for i in range(N):
                col = u * KR + j * N + i
                if u == 2 and j == 2:
                    c[XR - 1, col] = 1.0
                    continue
                f = slot[(i + j + (0, SHIFT, 2 * SHIFT - DOWN)[u]) % N]
                c[f, col] = c[SLOT + f, col] = 1.0
    for row in range(GR):
        f = slot[(row - DOWN) % N]
        c[f, NF * KR + row] = c[SLOT + f, NF * KR + row] = 1.0
    c[:, SELW:] = np.eye(P, dtype=np.float32)
    return c


_INS = ["r_dense_x", "r_discrete_x"] + ["L0_rec_" + n for n in (
    "lin_emb", "emb_W", "dense_W", "dense_b", "W1", "b1", "bn1_g", "bn1_b", "W2", "b2", "bn2_g", "bn2_b",
    "W3", "b3", "bn3_g", "bn3_b", "Wout", "bout", "dense_proj", "cin_W0", "cin_W1", "cin_W2",
    "cin_out_W", "cin_out_b")]


def kernel(**inputs):
    import numpy as _np
    import concourse.bacc as _bacc
    from concourse import mybir as _mybir
    from concourse.bass_utils import run_bass_kernel_spmd as _run

    nc = _bacc.Bacc("TRN2", target_bir_lowering=False, num_devices=1)
    arrays, args = {}, []
    for name in _INS + ["consts"]:
        a = _consts() if name == "consts" else _np.ascontiguousarray(inputs[name])
        arrays[f"in_{name}"] = a
        args.append(nc.dram_tensor(f"in_{name}", a.shape, _mybir.dt.from_np(a.dtype), kind="ExternalInput").ap())
    args.append(nc.dram_tensor("out_0", (B, 1), _mybir.dt.float32, kind="ExternalOutput").ap())
    build(nc, *args)
    r = _run(nc, [arrays], core_ids=[0])
    return r.results[0]["out_0"]
```
